# Optimizing a Trainium2 kernel written in Bass

```python
import numpy as np
import jax
import jax.numpy as jnp

def _softmax(x, axis=-1):
    return jax.nn.softmax(x, axis=axis)

def _gelu(x):
    return jax.nn.gelu(x, approximate=True)

def _silu(x):
    return jax.nn.silu(x)

def _sigmoid(x):
    return jax.nn.sigmoid(x)

def _layernorm(x, axis=-1, eps=1e-05):
    m = jnp.mean(x, axis=axis, keepdims=True)
    v = jnp.var(x, axis=axis, keepdims=True)
    return (x - m) / jnp.sqrt(v + eps)

def _scatter_add(tgt, idx, src, axis=0):
    return tgt.at[idx].add(src)

def _segment_sum(src, seg, n):
    return jax.ops.segment_sum(src, seg, n)
kernel_name = 'mk_lm_tower_d1_tok_ids1024_r4_b80dce'

def setup_inputs(seed: int=0):
    np.random.seed(seed)
    _w = jnp.asarray

    def _rec_inputs():
        import jax
        import jax.numpy as jnp
        _rk = jax.random.key(seed)
        x = jax.random.randint(jax.random.fold_in(_rk, 1), (32, 128), 0, 50226, jnp.int32)
        return x
    x = _rec_inputs()

    def _L0_tok_setup():
        import jax, jax.numpy as jnp
        import numpy as np
        B, T, D, H, L, V = (8, 256, 256, 16, 4, 50257)
        HD = D // H
        DF = 4 * D
        EPS = 1e-05

        def _layernorm(x, w, b):
            m = jnp.mean(x, axis=-1, keepdims=True)
            v = jnp.mean((x - m) ** 2, axis=-1, keepdims=True)
            return (x - m) * jax.lax.rsqrt(v + EPS) * w + b
        key = jax.random.key(seed)
        ks = jax.random.split(key, 17)
        s = 0.02
        n = lambda k, shape: (jax.random.normal(k, shape) * s).astype(jnp.float32)
        return {'idx': jax.random.randint(ks[0], (B, T), 0, V), 'tok_emb': n(ks[1], (V, D)), 'pos_emb': n(ks[2], (T, D)), 'wq': n(ks[3], (L, D, D)), 'wk': n(ks[4], (L, D, D)), 'wv': n(ks[5], (L, D, D)), 'w_proj': n(ks[6], (L, D, D)), 'b_proj': jnp.zeros((L, D), jnp.float32), 'ln1_w': jnp.ones((L, D), jnp.float32), 'ln1_b': jnp.zeros((L, D), jnp.float32), 'ln2_w': jnp.ones((L, D), jnp.float32), 'ln2_b': jnp.zeros((L, D), jnp.float32), 'w1': n(ks[7], (L, D, DF)), 'b1': jnp.zeros((L, DF), jnp.float32), 'w2': n(ks[8], (L, DF, D)), 'b2': jnp.zeros((L, D), jnp.float32)}
    _L0_tok_all = _L0_tok_setup()
    _L0_tok_in = {k: v for k, v in _L0_tok_all.items() if k in ('tok_emb', 'pos_emb', 'wq', 'wk', 'wv', 'w_proj', 'b_proj', 'ln1_w', 'ln1_b', 'ln2_w', 'ln2_b', 'w1', 'b1', 'w2', 'b2')}
    del _L0_tok_all

    def _L0_attn_setup():
        import jax, jax.numpy as jnp
        import numpy as np
        B, L, DIM, H, D = (4, 256, 256, 8, 32)
        key = jax.random.key(seed)
        ks = jax.random.split(key, 8)
        s = 0.02
        return dict(x=jax.random.normal(ks[0], (B, L, DIM), jnp.float32), W_in=jax.random.normal(ks[1], (DIM, DIM), jnp.float32) * s, b_in=jnp.zeros((DIM,), jnp.float32), W_qkva=jax.random.normal(ks[2], (H * D * 8, DIM), jnp.float32) * s, b_qkva=jnp.zeros((H * D * 8,), jnp.float32), W_y=jax.random.normal(ks[3], (DIM, H * D * 2), jnp.float32) * s, b_y=jnp.zeros((DIM,), jnp.float32), W_out=jax.random.normal(ks[4], (DIM, DIM), jnp.float32) * s, b_out=jnp.zeros((DIM,), jnp.float32), h0_re=jax.random.normal(ks[5], (H, D, D), jnp.float32), h0_im=jax.random.normal(ks[6], (H, D, D), jnp.float32))
    _L0_attn_all = _L0_attn_setup()
    _L0_attn_in = {k: v for k, v in _L0_attn_all.items() if k in ('W_in', 'b_in', 'W_qkva', 'b_qkva', 'W_y', 'b_y', 'W_out', 'b_out', 'h0_re', 'h0_im')}
    del _L0_attn_all

    def _L0_ffn_setup():
        import math
        import jax, jax.numpy as jnp
        import numpy as np
        B, S, D, F, E = (8, 512, 256, 1024, 8)
        CAPACITY_FACTOR = 1.0
        key = jax.random.key(seed)
        k1, k2, k3, k4 = jax.random.split(key, 4)
        x = jax.random.normal(k1, (B, S, D), dtype=jnp.float32)
        Wr = jax.random.normal(k2, (D, E), dtype=jnp.float32) * (1.0 / math.sqrt(D))
        W1 = jax.random.normal(k3, (E, D, F), dtype=jnp.float32) * (1.0 / math.sqrt(D))
        W2 = jax.random.normal(k4, (E, F, D), dtype=jnp.float32) * (1.0 / math.sqrt(F))
        return {'x': x, 'Wr': Wr, 'W1': W1, 'W2': W2}
    _L0_ffn_all = _L0_ffn_setup()
    _L0_ffn_in = {k: v for k, v in _L0_ffn_all.items() if k in ('Wr', 'W1', 'W2')}
    del _L0_ffn_all
    return {'x': x, 'L0_tok_tok_emb': _L0_tok_in['tok_emb'], 'L0_tok_pos_emb': _L0_tok_in['pos_emb'], 'L0_tok_wq': _L0_tok_in['wq'], 'L0_tok_wk': _L0_tok_in['wk'], 'L0_tok_wv': _L0_tok_in['wv'], 'L0_tok_w_proj': _L0_tok_in['w_proj'], 'L0_tok_b_proj': _L0_tok_in['b_proj'], 'L0_tok_ln1_w': _L0_tok_in['ln1_w'], 'L0_tok_ln1_b': _L0_tok_in['ln1_b'], 'L0_tok_ln2_w': _L0_tok_in['ln2_w'], 'L0_tok_ln2_b': _L0_tok_in['ln2_b'], 'L0_tok_w1': _L0_tok_in['w1'], 'L0_tok_b1': _L0_tok_in['b1'], 'L0_tok_w2': _L0_tok_in['w2'], 'L0_tok_b2': _L0_tok_in['b2'], 'L0_attn_W_in': _L0_attn_in['W_in'], 'L0_attn_b_in': _L0_attn_in['b_in'], 'L0_attn_W_qkva': _L0_attn_in['W_qkva'], 'L0_attn_b_qkva': _L0_attn_in['b_qkva'], 'L0_attn_W_y': _L0_attn_in['W_y'], 'L0_attn_b_y': _L0_attn_in['b_y'], 'L0_attn_W_out': _L0_attn_in['W_out'], 'L0_attn_b_out': _L0_attn_in['b_out'], 'L0_attn_h0_re': _L0_attn_in['h0_re'], 'L0_attn_h0_im': _L0_attn_in['h0_im'], 'L0_ffn_Wr': _L0_ffn_in['Wr'], 'L0_ffn_W1': _L0_ffn_in['W1'], 'L0_ffn_W2': _L0_ffn_in['W2']}

def reference(x, L0_tok_tok_emb, L0_tok_pos_emb, L0_tok_wq, L0_tok_wk, L0_tok_wv, L0_tok_w_proj, L0_tok_b_proj, L0_tok_ln1_w, L0_tok_ln1_b, L0_tok_ln2_w, L0_tok_ln2_b, L0_tok_w1, L0_tok_b1, L0_tok_w2, L0_tok_b2, L0_attn_W_in, L0_attn_b_in, L0_attn_W_qkva, L0_attn_b_qkva, L0_attn_W_y, L0_attn_b_y, L0_attn_W_out, L0_attn_b_out, L0_attn_h0_re, L0_attn_h0_im, L0_ffn_Wr, L0_ffn_W1, L0_ffn_W2):
    import jax
    import jax.numpy as jnp

    def _L0_tok_ref(idx, tok_emb, pos_emb, wq, wk, wv, w_proj, b_proj, ln1_w, ln1_b, ln2_w, ln2_b, w1, b1, w2, b2):
        import jax, jax.numpy as jnp
        import numpy as np
        B, T, D, H, L, V = (8, 256, 256, 16, 4, 50257)
        HD = D // H
        DF = 4 * D
        EPS = 1e-05

        def _layernorm(x, w, b):
            m = jnp.mean(x, axis=-1, keepdims=True)
            v = jnp.mean((x - m) ** 2, axis=-1, keepdims=True)
            return (x - m) * jax.lax.rsqrt(v + EPS) * w + b
        b, t = idx.shape
        x = tok_emb[idx] + pos_emb[:t]
        causal_mask = jnp.tril(jnp.ones((t, t), dtype=bool))
        scale = jnp.asarray(D, x.dtype) ** (-0.5)
        for l in range(L):
            h = _layernorm(x, ln1_w[l], ln1_b[l])
            q = (h @ wq[l]).reshape(b, t, H, HD)
            k = (h @ wk[l]).reshape(b, t, H, HD)
            v = (h @ wv[l]).reshape(b, t, H, HD)
            scores = jnp.einsum('bthd,bshd->bhts', q, k) * scale
            scores = jnp.where(causal_mask, scores, -jnp.inf)
            attn = jax.nn.softmax(scores, axis=-1)
            ctx = jnp.einsum('bhts,bshd->bthd', attn, v).reshape(b, t, D)
            x = x + (ctx @ w_proj[l] + b_proj[l])
            h2 = _layernorm(x, ln2_w[l], ln2_b[l])
            ff = jax.nn.relu(h2 @ w1[l] + b1[l]) @ w2[l] + b2[l]
            x = x + ff
        return x

    def _L0_attn_ref(x, W_in, b_in, W_qkva, b_qkva, W_y, b_y, W_out, b_out, h0_re, h0_im):
        import jax, jax.numpy as jnp
        import numpy as np
        B, L, DIM, H, D = (4, 256, 256, 8, 32)
        b, Ls, dim = x.shape
        Hh, Dd = (h0_re.shape[0], h0_re.shape[1])
        u = jax.nn.silu(x @ W_in.T + b_in)
        qkva = (u @ W_qkva.T + b_qkva).reshape(b, Ls, Hh, Dd, 4, 2)
        c = jax.lax.complex(qkva[..., 0], qkva[..., 1])
        q, k, v, a = (c[..., 0], c[..., 1], c[..., 2], c[..., 3])
        mag2 = a.real * a.real + a.imag * a.imag
        a = a * (jax.lax.rsqrt(mag2) * jax.nn.sigmoid(jnp.log(mag2)))
        kv = jnp.einsum('blhd,blhe->blhde', k, v)
        h0 = jax.lax.complex(h0_re, h0_im)[None]
        kv = kv.at[:, 0].add(a[:, 0, ..., None] * h0)
        a_e = a[..., None]

        def comb(c1, c2):
            a1, x1 = c1
            a2, x2 = c2
            return (a1 * a2, a2 * x1 + x2)
        _, h = jax.lax.associative_scan(comb, (a_e, kv), axis=1)
        y = jnp.einsum('blhd,blhde->blhe', q, h)
        y2 = jnp.stack([y.real, y.imag], axis=-1).reshape(b, Ls, Hh * Dd * 2)
        y2 = jax.nn.silu(y2 @ W_y.T + b_y)
        return y2 @ W_out.T + b_out

    def _L0_ffn_ref(x, Wr, W1, W2):
        import math
        import jax, jax.numpy as jnp
        import numpy as np
        B, S, D, F, E = (8, 512, 256, 1024, 8)
        CAPACITY_FACTOR = 1.0
        b, s, d = x.shape
        t = b * s
        cap = max(math.ceil(t * CAPACITY_FACTOR / E), 1)
        xf = x.reshape(t, d)
        probs = jax.nn.softmax(xf.astype(jnp.float32) @ Wr, axis=-1)
        eidx = jnp.argmax(probs, axis=-1)
        p_tok = jnp.take_along_axis(probs, eidx[:, None], axis=1)[:, 0]
        onehot = jax.nn.one_hot(eidx, E, dtype=jnp.int32)
        rank_all = jnp.cumsum(onehot, axis=0) - onehot
        rank = jnp.take_along_axis(rank_all, eidx[:, None], axis=1)[:, 0]
        keep = rank < cap
        slot = jnp.where(keep, rank, cap)
        dispatch = jnp.zeros((E, cap + 1), dtype=jnp.int32).at[eidx, slot].set(jnp.arange(t, dtype=jnp.int32))
        valid = jnp.zeros((E, cap + 1), dtype=bool).at[eidx, slot].set(keep)
        dispatch = dispatch[:, :cap]
        valid = valid[:, :cap]
        xe = xf[dispatch]
        h = jnp.maximum(jnp.einsum('ecd,edf->ecf', xe, W1), 0.0)
        ye = jnp.einsum('ecf,efd->ecd', h, W2)
        pe = p_tok[dispatch]
        ye = ye * (pe * valid.astype(ye.dtype))[:, :, None]
        y = jnp.zeros((t, d), dtype=x.dtype).at[dispatch.reshape(-1)].add(ye.reshape(E * cap, d).astype(x.dtype))
        return y.reshape(b, s, d)
    h = _L0_tok_ref(x, L0_tok_tok_emb, L0_tok_pos_emb, L0_tok_wq, L0_tok_wk, L0_tok_wv, L0_tok_w_proj, L0_tok_b_proj, L0_tok_ln1_w, L0_tok_ln1_b, L0_tok_ln2_w, L0_tok_ln2_b, L0_tok_w1, L0_tok_b1, L0_tok_w2, L0_tok_b2)
    h = h + _L0_attn_ref(_layernorm(h, axis=-1), L0_attn_W_in, L0_attn_b_in, L0_attn_W_qkva, L0_attn_b_qkva, L0_attn_W_y, L0_attn_b_y, L0_attn_W_out, L0_attn_b_out, L0_attn_h0_re, L0_attn_h0_im)
    h = h + _L0_ffn_ref(_layernorm(h, axis=-1), L0_ffn_Wr, L0_ffn_W1, L0_ffn_W2)
    return h

_drawn_inputs = setup_inputs


def setup_inputs(seed=0):
    import zlib

    import numpy as np

    out = dict(_drawn_inputs(seed))
    spreads = {'L0_tok_b_proj': (0.0, 0.1),
     'L0_tok_ln1_w': (1.0, 0.2),
     'L0_tok_ln1_b': (0.0, 0.1),
     'L0_tok_ln2_w': (1.0, 0.2),
     'L0_tok_ln2_b': (0.0, 0.1),
     'L0_tok_b1': (0.0, 0.1),
     'L0_tok_b2': (0.0, 0.1),
     'L0_attn_b_in': (0.0, 0.8),
     'L0_attn_b_qkva': (0.0, 0.78),
     'L0_attn_b_y': (0.0, 2.0),
     'L0_attn_b_out': (0.0, 2.0)}
    factors = {'L0_tok_wq': 3.493,
     'L0_tok_wk': 3.723,
     'L0_attn_W_in': 3.839,
     'L0_attn_W_qkva': 5.966,
     'L0_attn_W_y': 3.268,
     'L0_attn_h0_re': 8.0,
     'L0_attn_h0_im': 8.0,
     'L0_ffn_Wr': 8.0,
     'L0_ffn_W1': 8.0,
     'L0_ffn_W2': 8.0}
    for name, (base, spread) in spreads.items():
        noise = np.random.default_rng([zlib.crc32(name.encode()), seed]).standard_normal(out[name].shape)
        drawn = base * np.exp(spread * noise) if base else spread * noise
        out[name] = jnp.asarray(drawn.astype(out[name].dtype))
    for name, factor in factors.items():
        out[name] = (out[name] * factor).astype(out[name].dtype)
    return out
```

```python
from contextlib import ExitStack

import concourse.bass as bass
from concourse import mybir

F32 = mybir.dt.float32
BF16 = mybir.dt.bfloat16
I32 = mybir.dt.int32
U32 = mybir.dt.uint32
ALU = mybir.AluOpType
ACT = mybir.ActivationFunctionType
AX = mybir.AxisListType

P = 128
B, T, D = 32, 128, 256
KC = D // P
LAYERS, HEADS = 4, 16
HD = D // HEADS
HV = HD + 1
FF = 4 * D
FC = FF // P
G = 4
STEPS_L = B // G
STEPS = LAYERS * STEPS_L
GT = G * T
UNITS = 4 * G
EPS = 1e-5
MASKED = -1e30
RSQRT_MAGIC = 0x5F3759DF


def at_least(eng, sem, value):
    if isinstance(value, int) and value <= 0:
        return
    eng.wait_ge(sem, value)


class Step:

    def __init__(self, kind, i):
        self.kind, self.i = kind, i


def step_uses(kind):
    uses = [("T1", 0), ("T1", 1), ("Q", 0), ("Q", 1), ("K", 0), ("K", 1), ("V", 0), ("V", 1), ("T2", 0), ("T2", 1)]
    for u in range(UNITS):
        if u < FC:
            uses.append(("F1", u))
        elif u % 2 == 0:
            uses.append(("F2", (u - FC) // 2))
        if u >= 6 and u % 4 == 2:
            uses.append(("CT", (u - 6) // 4))
        if u >= 7 and u % 4 == 3:
            uses.append(("PJ", (u - 7) // 4))
    uses += [("CT", G - 1), ("PJ", G - 1)]
    attn = ("T1", "Q", "K", "V", "CT", "PJ")
    return [u if kind == "body" or (u[0] in attn) == (kind == "first") else None for u in uses]


NBANK = 3
GATHERS = 4


def bank_of(step, name, idx):
    uses = step_uses(step.kind)
    at = uses.index((name, idx))
    bank = at % NBANK
    before = sum(1 for n in range(bank, at, NBANK) if uses[n] is not None)
    if step.kind == "first":
        return bank, before
    firsts = sum(1 for n in range(bank, len(uses), NBANK) if step_uses("first")[n] is not None)
    per = len(uses) // NBANK
    assert len(uses) % NBANK == 0
    return bank, firsts + (step.i - 1) * per + before


def norm_group(dve, link, x_sb, g, dst, done, small):
    stats, means, rstd, scratch, varc = small
    for t in range(G):
        last = dve.bn_stats(stats[:, t, :], x_sb[:, g * G + t, :])
    link(last)
    rs, sc, va, mean = rstd[:, :, 0], scratch[:, :, 0], varc[:, :, 0], means[:, :, 0]
    dve.tensor_tensor(mean, stats[:, :, 1], stats[:, :, 4], ALU.add)
    dve.tensor_tensor(sc, stats[:, :, 1], stats[:, :, 4], ALU.subtract)
    link(dve.tensor_tensor(va, stats[:, :, 2], stats[:, :, 5], ALU.add))
    dve.tensor_scalar(mean, mean, 0.5, None, ALU.mult)
    link(dve.scalar_tensor_tensor(sc, sc, 0.25, sc, ALU.mult, ALU.mult))
    link(dve.scalar_tensor_tensor(va, va, 1.0 / D, sc, ALU.mult, ALU.add))
    link(dve.tensor_scalar(va, va, EPS, None, ALU.add))
    link(dve.tensor_scalar(sc.bitcast(I32), va.bitcast(I32), 1, None, ALU.logical_shift_right))
    link(dve.tensor_scalar(rs.bitcast(I32), sc.bitcast(I32), -1.0, float(RSQRT_MAGIC), ALU.mult, ALU.add))
    for _ in range(3):
        link(dve.scalar_tensor_tensor(sc, rs, -0.5, rs, ALU.mult, ALU.mult))
        link(dve.tensor_tensor(sc, sc, va, ALU.mult))
        link(dve.scalar_tensor_tensor(rs, sc, 1.5, rs, ALU.add, ALU.mult))
    for t in range(G):
        last = dve.tensor_scalar(dst[:, t, :], x_sb[:, g * G + t, :], means[:, t, :], rstd[:, t, :],
                                 ALU.subtract, ALU.mult)
    last.then_inc(done, 1)


def transformer(nc, ctx, x_sb, ins, consts):
    def sb(name, shape, dt=F32):
        return ctx.enter_context(nc.sbuf_tensor(name, shape, dt))

    def sem(name):
        return ctx.enter_context(nc.semaphore(name))

    ident, ident16, causal, half_masks = consts

    wqkv = sb("wqkv", [P, KC, 3 * D])
    wproj = sb("wproj", [P, KC, D])
    w1 = sb("w1", [P, KC, FF])
    w2 = sb("w2", [P, FC, D])
    ln1 = sb("ln1", [P, 2 * KC])
    ln2 = sb("ln2", [P, 2 * KC])
    b1 = sb("b1", [P, FC])
    bproj = sb("bproj", [P, D])
    b2 = sb("b2", [P, D])

    causal32 = sb("causal32", [P, T])
    idx = sb("idx", [P, B], I32)
    pos = sb("pos", [P, D])
    xhat1 = sb("xhat1", [P, G, D])
    xhat2 = sb("xhat2", [P, G, D])
    stats = sb("stats", [P, G, 6])
    means = sb("means", [P, G, 1])
    rstd = sb("rstd", [P, G, 1])
    scratch = sb("scratch", [P, G, 1])
    varc = sb("varc", [P, G, 1])
    x1T = sb("x1T", [P, KC, GT])
    x2T = sb("x2T", [P, KC, GT])
    qT = sb("qT", [P, KC, GT])
    kT = sb("kT", [P, KC, 2, GT])
    v1 = sb("v1", [P, G, HEADS, HV])
    rowmax = sb("rowmax", [P, 2, 4])
    shifted = sb("shifted", [P, 2, 4 * T])
    probs = sb("probs", [P, 2, 4 * T])
    probsT = sb("probsT", [P, 2, 4 * T])
    rsum = sb("rsum", [P, HEADS])
    ctx_sb = sb("ctx_sb", [P, 2, D])
    ctxT = sb("ctxT", [P, 2, KC, T])
    hidT = sb("hidT", [P, FC, GT])

    def bank(name):
        return ctx.enter_context(nc.psum_tensor(name, [P, 512], F32))

    ps_scores = [bank(f"ps_scores{n}") for n in range(2)]
    ps_probsT = [bank(f"ps_probsT{n}") for n in range(2)]
    ps_ctx = bank("ps_ctx")
    ps_mm = [bank(f"ps_mm{n}") for n in range(NBANK)]

    consts_in = sem("consts_in")
    idx_in = sem("idx_in")
    rows_in = [sem(f"rows_in{n}") for n in range(GATHERS)]
    embedded = sem("embedded")
    attn_w_in = sem("attn_w_in")
    ffn_w_in = sem("ffn_w_in")
    mm_ready = [sem(f"mm_ready{n}") for n in range(NBANK)]
    mm_taken = [sem(f"mm_taken{n}") for n in range(NBANK)]
    ones_set = sem("ones_set")
    masks_cast = sem("masks_cast")
    ln1_done = sem("ln1_done")
    ln2_done = sem("ln2_done")
    bproj_added = sem("bproj_added")
    b2_added = sem("b2_added")
    scores_ready = sem("scores_ready")
    scores_taken = sem("scores_taken")
    probs_ready = sem("probs_ready")
    probsT_ready = sem("probsT_ready")
    probsT_taken = sem("probsT_taken")
    pv_done = sem("pv_done")
    ctx_taken = sem("ctx_taken")
    dve_chain = sem("dve_chain")

    N_ATTN_W, N_FFN_W, N_CONST = 6, 5, 3
    x_tok = ins["tok_emb"]
    block = ctx.enter_context(nc.Block())

    def layer_of(i):
        return i // STEPS_L

    def group(i):
        return i % STEPS_L

    @block.sync
    def _(sp):
        sp.dma_start(idx[:, :], ins["idxT"]).then_inc(idx_in, 16)
        sp.dma_start(pos[:, :], ins["pos_emb"][0:T, :]).then_inc(idx_in, 16)
        sp.dma_start(ident[:, :], ins["ident"]).then_inc(consts_in, 16)
        sp.dma_start(causal32[:, :], ins["causal"]).then_inc(consts_in, 16)
        sp.dma_start(half_masks[:, :], ins["half_masks"]).then_inc(consts_in, 16)

        def row_bcast(name, l):
            return ins[name][bass.ds(l, 1), :].to_broadcast([P, D])

        def load_attn(l):
            for n, w in enumerate(("wq", "wk", "wv")):
                sp.dma_start(wqkv[:, :, n * D:(n + 1) * D],
                             ins[w][bass.ds(l, 1)].rearrange("a (c p) n -> p (a c) n", p=P)).then_inc(attn_w_in, 16)
            sp.dma_start(wproj[:, :, :],
                         ins["w_proj"][bass.ds(l, 1)].rearrange("a (c p) n -> p (a c) n", p=P)).then_inc(attn_w_in, 16)
            sp.dma_start(ln1[:, :], ins["ln1_cols"][bass.ds(l, 1)].rearrange("a p n -> (a p) n")).then_inc(attn_w_in, 16)
            sp.dma_start(bproj[:, :], row_bcast("b_proj", l)).then_inc(attn_w_in, 16)

        def load_ffn(l):
            sp.dma_start(ln2[:, :], ins["ln2_cols"][bass.ds(l, 1)].rearrange("a p n -> (a p) n")).then_inc(ffn_w_in, 16)
            sp.dma_start(w1[:, :, :],
                         ins["w1"][bass.ds(l, 1)].rearrange("a (c p) n -> p (a c) n", p=P)).then_inc(ffn_w_in, 16)
            sp.dma_start(w2[:, :, :],
                         ins["w2"][bass.ds(l, 1)].rearrange("a (c p) n -> p (a c) n", p=P)).then_inc(ffn_w_in, 16)
            sp.dma_start(b1[:, :], ins["b1_cols"][bass.ds(l, 1)].rearrange("a p n -> (a p) n")).then_inc(ffn_w_in, 16)
            sp.dma_start(b2[:, :], row_bcast("b2", l)).then_inc(ffn_w_in, 16)

        load_attn(0)
        load_ffn(0)
        with sp.Fori(1, LAYERS) as l:
            n, before = bank_of(Step("body", l * STEPS_L - 1), "PJ", G - 1)
            sp.wait_ge(mm_ready[n], before + 1)
            sp.wait_ge(bproj_added, l * STEPS_L)
            load_attn(l)
            n, before = bank_of(Step("body", l * STEPS_L), "F2", G - 1)
            sp.wait_ge(mm_ready[n], before + 1)
            sp.wait_ge(b2_added, l * STEPS_L)
            load_ffn(l)

    @block.gpsimd
    def _(pool):
        pool.memset(v1[:, :, :, HD:HV].rearrange("p g h o -> p (g h) o"), 1.0).then_inc(ones_set, 1)
        pool.wait_ge(idx_in, 32)

        def gather(b, n):
            pool.indirect_dma_start(out=x_sb[:, b, :], out_offset=None, in_=x_tok[:, :],
                                    in_offset=bass.IndirectOffsetOnAxis(ap=idx[:, b:b + 1], axis=0)
                                    ).then_inc(rows_in[n], 16)

        def add_pos(b, n):
            pool.wait_ge(rows_in[n], 16 * (b // GATHERS + 1))
            pool.tensor_tensor(x_sb[:, b, :], x_sb[:, b, :], pos[:, :], ALU.add).then_inc(embedded, 1)

        for b in range(GATHERS):
            gather(b, b)
        for b in range(B):
            add_pos(b, b % GATHERS)
            if b + GATHERS < B:
                gather(b + GATHERS, b % GATHERS)

        def bproj_add(i):
            xg = x_sb[:, bass.ds(group(i) * G, G), :]
            pool.wait_ge(attn_w_in, 16 * N_ATTN_W * (layer_of(i) + 1))
            pool.wait_ge(ln1_done, i + 1)
            pool.tensor_tensor(xg, xg, bproj[:, :].unsqueeze(1).to_broadcast([P, G, D]), ALU.add).then_inc(bproj_added, 1)

        def b2_add(i):
            xg = x_sb[:, bass.ds(group(i) * G, G), :]
            pool.wait_ge(ffn_w_in, 16 * N_FFN_W * (layer_of(i) + 1))
            pool.wait_ge(ln2_done, i + 1)
            pool.tensor_tensor(xg, xg, b2[:, :].unsqueeze(1).to_broadcast([P, G, D]), ALU.add).then_inc(b2_added, 1)

        bproj_add(0)
        with pool.Fori(1, STEPS) as i:
            b2_add(i - 1)
            bproj_add(i)
        b2_add(STEPS - 1)

    @block.tensor
    def _(pe):
        def open_bank(step, name, idx):
            n, before = bank_of(step, name, idx)
            at_least(pe, mm_taken[n], before)
            return ps_mm[n], mm_ready[n]

        def turn(step, name, src, done):
            for c in range(KC):
                ps, ready = open_bank(step, name, c)
                if c == 0:
                    pe.wait_ge(*done)
                for t in range(G):
                    mm = pe.transpose(ps[:, t * T:(t + 1) * T], src[:, t, c * P:(c + 1) * P], ident[:, :])
                mm.then_inc(ready, 1)

        def taken(step, name, idx):
            n, before = bank_of(step, name, idx)
            pe.wait_ge(mm_taken[n], before + 1)

        def qkv(step):
            i = step.i
            pe.wait_ge(attn_w_in, 16 * N_ATTN_W * (layer_of(i) + 1))
            taken(step, "T1", 1)
            for w, name in enumerate(("Q", "K")):
                for m in range(KC):
                    ps, ready = open_bank(step, name, m)
                    for c in range(KC):
                        mm = pe.matmul(ps[:, :], wqkv[:, c, w * D + m * P:w * D + (m + 1) * P], x1T[:, c, :],
                                       start=(c == 0), stop=(c == KC - 1))
                    mm.then_inc(ready, 1)
            for n in range(2):
                ps, ready = open_bank(step, "V", n)
                for t in range(2):
                    for c in range(KC):
                        mm = pe.matmul(ps[:, t * D:(t + 1) * D], x1T[:, c, (2 * n + t) * T:(2 * n + t + 1) * T],
                                       wqkv[:, c, 2 * D:3 * D], start=(c == 0), stop=(c == KC - 1))
                mm.then_inc(ready, 1)

        def scores(step, u):
            i, t, q = step.i, u // 4, u % 4
            ps = ps_scores[u % 2]
            pe.matmul(ps[:, :], ident16[:, :], causal[:, :, :], start=True, stop=False)
            rows = slice(32 * q, 32 * q + 32)
            for m in range(KC):
                mm = pe.matmul(ps[:, m * 2 * T:(m + 1) * 2 * T], qT[rows, m, t * T:(t + 1) * T],
                               kT[rows, m, :, t * T:(t + 1) * T], start=False, stop=(m == KC - 1))
            mm.then_inc(scores_ready, 1)

        def turn_probs(step, u):
            i = step.i
            pe.wait_ge(probs_ready, UNITS * i + u + 1)
            for c in range(4):
                mm = pe.transpose(ps_probsT[u % 2][:, c * T:(c + 1) * T], probs[:, u % 2, c * T:(c + 1) * T], ident[:, :])
            mm.then_inc(probsT_ready, 1)

        def values(step, u):
            i, t, q = step.i, u // 4, u % 4
            pe.wait_ge(probsT_taken, UNITS * i + u + 1)
            if q == 0:
                at_least(pe, ctx_taken, G * i + t)
            for c in range(4):
                h = (c // 2) * (HEADS // 2) + 2 * q + c % 2
                mm = pe.matmul(ps_ctx[:, h * HV:(h + 1) * HV], probsT[:, u % 2, c * T:(c + 1) * T], v1[:, t, h, :],
                               start=True, stop=True)
            mm.then_inc(pv_done, 1)

        def turn_ctx(step, t):
            ps, ready = open_bank(step, "CT", t)
            pe.wait_ge(ctx_taken, G * step.i + t + 1)
            for c in range(KC):
                mm = pe.transpose(ps[:, c * T:(c + 1) * T], ctx_sb[:, t % 2, c * P:(c + 1) * P], ident[:, :])
            mm.then_inc(ready, 1)

        def project(step, t):
            ps, ready = open_bank(step, "PJ", t)
            taken(step, "CT", t)
            for c in range(KC):
                mm = pe.matmul(ps[:, 0:D], ctxT[:, t % 2, c, :], wproj[:, c, :], start=(c == 0), stop=(c == KC - 1))
            mm.then_inc(ready, 1)

        def ffn_piece(step, u):
            i = step.i
            if u < FC:
                ps, ready = open_bank(step, "F1", u)
                if u == 0:
                    pe.wait_ge(ffn_w_in, 16 * N_FFN_W * (layer_of(i - 1) + 1))
                    taken(step, "T2", 1)
                for c in range(KC):
                    mm = pe.matmul(ps[:, :], w1[:, c, u * P:(u + 1) * P], x2T[:, c, :], start=(c == 0), stop=(c == KC - 1))
                mm.then_inc(ready, 1)
                return
            t, half = (u - FC) // 2, u % 2
            if half == 0:
                open_bank(step, "F2", t)
                if t == 0:
                    taken(step, "F1", FC - 1)
            n, _ = bank_of(step, "F2", t)
            for f in range(4 * half, 4 * half + 4):
                mm = pe.matmul(ps_mm[n][:, 0:D], hidT[:, f, t * T:(t + 1) * T], w2[:, f, :],
                               start=(f == 0), stop=(f == FC - 1))
            if half == 1:
                mm.then_inc(mm_ready[n], 1)

        def run(step):
            i, attn, ffn = step.i, step.kind != "last", step.kind != "first"
            if attn:
                turn(step, "T1", xhat1, (ln1_done, i + 1))
                qkv(step)
            if ffn:
                turn(step, "T2", xhat2, (ln2_done, i))
            if attn:
                taken(step, "Q", 1)
                taken(step, "K", 1)
                scores(step, 0)
                scores(step, 1)
                taken(step, "V", 1)
            for u in range(UNITS):
                if ffn:
                    ffn_piece(step, u)
                if attn:
                    turn_probs(step, u)
                    if u + 2 < UNITS:
                        scores(step, u + 2)
                    if u >= 1:
                        values(step, u - 1)
                    if u >= 6 and u % 4 == 2:
                        turn_ctx(step, (u - 6) // 4)
                    if u >= 7 and u % 4 == 3:
                        project(step, (u - 7) // 4)
            if attn:
                values(step, UNITS - 1)
                turn_ctx(step, G - 1)
                project(step, G - 1)

        pe.wait_ge(consts_in, 16 * N_CONST)
        pe.wait_ge(masks_cast, 1)
        pe.wait_ge(ones_set, 1)
        run(Step("first", 0))
        with pe.Fori(1, STEPS) as i:
            run(Step("body", i))
        run(Step("last", STEPS))

    @block.scalar
    def _(act):
        def take(step, name, idx):
            n, before = bank_of(step, name, idx)
            act.wait_ge(mm_ready[n], before + 1)
            return ps_mm[n], mm_taken[n]

        def scale_turned(step, name, ln, dst):
            for c in range(KC):
                ps, taken = take(step, name, c)
                act.activation(dst[:, c, :], ps[:, :], ACT.Identity, bias=ln[:, KC + c:KC + c + 1],
                               scale=ln[:, c:c + 1]).then_inc(taken, 1)

        def keys(step):
            for m in range(KC):
                ps, taken = take(step, "K", m)
                act.activation(kT[:, m, 0, :], ps[:, :], ACT.Copy, scale=half_masks[:, 0:1])
                act.activation(kT[:, m, 1, :], ps[:, :], ACT.Copy, scale=half_masks[:, 1:2]).then_inc(taken, 1)

        def exps(step, u):
            i = step.i
            act.wait_ge(scores_taken, UNITS * i + u + 1)
            act.activation(probs[:, u % 2, :], shifted[:, u % 2, :], ACT.Exp, scale=float(D) ** -0.5).then_inc(probs_ready, 1)

        def take_probsT(step, u):
            i = step.i
            act.wait_ge(probsT_ready, UNITS * i + u + 1)
            act.activation(probsT[:, u % 2, :], ps_probsT[u % 2][:, :], ACT.Copy).then_inc(probsT_taken, 1)

        def take_ctx(step, t):
            ps, taken = take(step, "CT", t)
            act.activation(ctxT[:, t % 2, :, :].rearrange("p c t -> p (c t)"), ps[:, 0:D], ACT.Copy).then_inc(taken, 1)

        def hidden(step, c):
            ps, taken = take(step, "F1", c)
            act.activation(hidT[:, c, :], ps[:, :], ACT.Relu, bias=b1[:, c:c + 1]).then_inc(taken, 1)

        def run(step):
            i, attn, ffn = step.i, step.kind != "last", step.kind != "first"
            if attn:
                act.wait_ge(attn_w_in, 16 * N_ATTN_W * (layer_of(i) + 1))
                scale_turned(step, "T1", ln1, x1T)
                keys(step)
            if ffn:
                act.wait_ge(ffn_w_in, 16 * N_FFN_W * (layer_of(i - 1) + 1))
                scale_turned(step, "T2", ln2, x2T)
            if attn:
                exps(step, 0)
            for u in range(UNITS):
                if ffn and u < FC:
                    hidden(step, u)
                if attn:
                    if u + 1 < UNITS:
                        exps(step, u + 1)
                    take_probsT(step, u)
                    if u >= 6 and u % 4 == 2:
                        take_ctx(step, (u - 6) // 4)
            if attn:
                take_ctx(step, G - 1)

        act.wait_ge(consts_in, 16 * N_CONST)
        run(Step("first", 0))
        with act.Fori(1, STEPS) as i:
            run(Step("body", i))
        run(Step("last", STEPS))

    LINKS_STEP = 2 * 16 + UNITS + G

    @block.vector
    def _(dve):
        links, before_step = [0], [0]

        def link(ins):
            links[0] += 1
            ins.then_inc(dve_chain, 1)
            dve.wait_ge(dve_chain, before_step[0] + links[0])

        def take(step, name, idx):
            n, before = bank_of(step, name, idx)
            dve.wait_ge(mm_ready[n], before + 1)
            return ps_mm[n], mm_taken[n]

        def norm(i, dst, done):
            norm_group(dve, link, x_sb, group(i), dst, done, (stats, means, rstd, scratch, varc))

        def norm1(i, rows):
            dve.wait_ge(embedded, rows)
            norm(i, xhat1, ln1_done)

        def norm2(step):
            n, per = (len(step_uses("body")) - 1) % NBANK, len(step_uses("body")) // NBANK
            firsts = sum(1 for at, use in enumerate(step_uses("first")) if use and at % NBANK == n)
            dve.wait_ge(mm_taken[n], firsts + (step.i - 1) * per)
            norm(step.i - 1, xhat2, ln2_done)

        def softmax_shift(step, u):
            i = step.i
            ps = ps_scores[u % 2][:, :].rearrange("p (h s) -> p h s", h=4)
            mx = rowmax[:, u % 2, :]
            dve.wait_ge(scores_ready, UNITS * i + u + 1)
            link(dve.tensor_reduce(mx, ps, AX.X, ALU.max))
            dve.tensor_tensor(shifted[:, u % 2, :].rearrange("p (h s) -> p h s", h=4), ps,
                              mx.unsqueeze(2).to_broadcast([P, 4, T]), ALU.subtract).then_inc(scores_taken, 1)

        def take_context(step, t):
            i = step.i
            dve.wait_ge(pv_done, UNITS * i + 4 * t + 4)
            ps = ps_ctx[:, 0:HEADS * HV].rearrange("p (h v) -> p h v", v=HV)
            link(dve.reciprocal(rsum[:, :], ps[:, :, HD]))
            dve.tensor_tensor(ctx_sb[:, t % 2, :].rearrange("p (h v) -> p h v", v=HD), ps[:, :, 0:HD],
                              rsum[:, :].unsqueeze(2).to_broadcast([P, HEADS, HD]), ALU.mult).then_inc(ctx_taken, 1)

        def add_projection(step, t):
            xt = x_sb[:, group(step.i) * G + t, :]
            ps, taken = take(step, "PJ", t)
            if t == 0:
                dve.wait_ge(bproj_added, step.i + 1)
            dve.tensor_tensor(xt, ps[:, 0:D], xt, ALU.add).then_inc(taken, 1)

        def add_ffn(step, t):
            xt = x_sb[:, group(step.i - 1) * G + t, :]
            ps, taken = take(step, "F2", t)
            if t == 0:
                dve.wait_ge(b2_added, step.i)
            dve.tensor_tensor(xt, ps[:, 0:D], xt, ALU.add).then_inc(taken, 1)

        def run(step):
            i, attn, ffn = step.i, step.kind != "last", step.kind != "first"
            if attn:
                for m in range(KC):
                    ps, taken = take(step, "Q", m)
                    dve.tensor_copy(qT[:, m, :], ps[:, :]).then_inc(taken, 1)
            if ffn:
                norm2(step)
            if attn:
                for n in range(2):
                    ps, taken = take(step, "V", n)
                    dve.tensor_copy(v1[:, 2 * n:2 * n + 2, :, 0:HD].rearrange("p t h v -> p (t h) v"),
                                    ps[:, :].rearrange("p (h v) -> p h v", v=HD)).then_inc(taken, 1)
                softmax_shift(step, 0)
            for u in range(UNITS):
                if attn:
                    if u + 1 < UNITS:
                        softmax_shift(step, u + 1)
                    if u >= 5 and u % 4 == 1:
                        take_context(step, (u - 5) // 4)
                    if u >= 8 and u % 4 == 0:
                        add_projection(step, (u - 8) // 4)
                    if u == 9:
                        norm1(i + 1, 2 * G if step.kind == "first" else B)
                if ffn and u >= FC and u % 2 == 1:
                    add_ffn(step, (u - FC) // 2)
            if attn:
                add_projection(step, G - 2)
                take_context(step, G - 1)
                add_projection(step, G - 1)

        dve.wait_ge(consts_in, 16 * N_CONST)
        dve.tensor_copy(ident16[:, :], ident[:, :])
        dve.tensor_copy(causal[:, :, :], causal32[:, :].unsqueeze(1).to_broadcast([P, 4, T])).then_inc(masks_cast, 1)
        norm1(0, G)
        run(Step("first", 0))
        head, links[0] = links[0], 0
        with dve.Fori(1, STEPS) as i:
            before_step[0] = head + (i - 1) * LINKS_STEP
            run(Step("body", i))
        assert links[0] == LINKS_STEP
        before_step[0], links[0] = head + (STEPS - 1) * LINKS_STEP, 0
        run(Step("last", STEPS))


class Banks:

    def __init__(self, nc, ctx, tag, uses, n=8):
        self.ps = [ctx.enter_context(nc.psum_tensor(f"ps_{tag}{k}", [P, 512], F32)) for k in range(n)]
        self.ready = [ctx.enter_context(nc.semaphore(f"{tag}_ready{k}")) for k in range(n)]
        self.taken = [ctx.enter_context(nc.semaphore(f"{tag}_taken{k}")) for k in range(n)]
        self.at = {use: k for k, use in enumerate(uses)}
        self.uses, self.n = uses, n
        self.per = [len(range(k, len(uses), n)) for k in range(n)]

    def count(self, use, r):
        k = self.at[use]
        return k % self.n, r * self.per[k % self.n] + k // self.n


LA_HEADS, LA_D = 8, 32
LEVELS = [1, 2, 4, 8, 16, 32, 64]
MASK_LEVELS = 5
COMPS = ["are", "aim", "kre", "kim", "qre", "qim"]
TILES = LA_HEADS // 2
LA_ROUNDS = B // G


def linear_attention(nc, ctx, x_sb, ins, consts):
    def sb(name, shape, dt=F32):
        return ctx.enter_context(nc.sbuf_tensor(name, shape, dt))

    def sem(name):
        return ctx.enter_context(nc.semaphore(name))

    ident = consts[0]
    N2 = KC * GT

    w_in = sb("w_in", [P, KC, D])
    w_comp = sb("w_comp", [P, KC, len(COMPS) * D])
    w_v = sb("w_v", [P, KC, 2 * D])
    w_y = sb("w_y", [P, 2 * KC, D])
    w_out = sb("w_out", [P, KC, D])
    h0 = sb("h0", [P, TILES, 2 * LA_D])
    bias_cols = sb("bias_cols", [P, 2 * len(COMPS) + 2 * KC])
    v_bias = sb("v_bias", [P, 2 * D])
    out_bias = sb("out_bias", [P, D])
    level_masks = sb("level_masks", [P, MASK_LEVELS, T // 2], U32)

    stats = sb("la_stats", [P, G, 6])
    means = sb("la_means", [P, G, 1])
    rstd = sb("la_rstd", [P, G, 1])
    scratch = sb("la_scratch", [P, G, 1])
    varc = sb("la_varc", [P, G, 1])

    arena = sb("arena", [P, 8 * N2])
    tmp = [arena[:, n * N2:(n + 1) * N2] for n in range(4)]
    raw = {name: arena[:, (4 + n) * N2:(5 + n) * N2] for n, name in enumerate(("are", "aim", "qre", "qim"))}
    s_all = arena[:, :].rearrange("p (h g r t) -> p h g r t", h=LA_HEADS, g=G, r=2)
    arena2 = sb("arena2", [P, 2 * N2])
    raw["kre"], raw["kim"] = arena2[:, 0:N2], arena2[:, N2:2 * N2]
    yT = arena2[:, :].rearrange("p (c t) -> p c t", c=2 * KC)
    arena3 = sb("arena3", [P, 2 * N2])
    xhat = arena3[:, 0:N2].rearrange("p (g d) -> p g d", g=G)
    xT = arena3[:, N2:2 * N2].rearrange("p (c t) -> p c t", c=KC)
    y_sb = arena3[:, :].rearrange("p (g d) -> p g d", g=G)
    uT = sb("uT", [P, KC, GT])
    decay = sb("decay", [P, N2])
    neg_qim = sb("neg_qim", [P, N2])
    q12 = sb("q12", [P, 2, TILES, GT])
    k12 = sb("k12", [P, TILES, GT])
    totals = sb("totals", [P, 2 * TILES * GT])
    v_sb = sb("v_sb", [P, G, LA_HEADS, 3 * LA_D])

    def total(m):
        n = TILES * GT
        at = 2 * n - 2 * n // m
        return totals[:, at:at + n // m]

    uses = [("T", c) for c in range(KC)] + [("U", m) for m in range(KC)]
    uses += [(comp, m) for comp in COMPS for m in range(KC)] + [("V", g) for g in range(G)]
    uses += [("D", h, pair) for h in range(LA_HEADS) for pair in range(2)]
    uses += [("S", m, h) for m in LEVELS for h in range(LA_HEADS)]
    uses += [("Y", g) for g in range(G)] + [("YT", g) for g in range(G)]
    uses += [("Z", m) for m in range(KC)] + [("O", g) for g in range(G)]
    banks = Banks(nc, ctx, "la", uses)

    weights_in = sem("la_weights_in")
    ln_done = sem("la_ln_done")
    bias_added = sem("la_bias_added")
    mag_ready = sem("mag_ready")
    root_ready = sem("root_ready")
    decay_ready = sem("decay_ready")
    q_ready = sem("q_ready")
    k_ready = sem("k_ready")
    negq_ready = sem("negq_ready")
    decay_stacked = sem("decay_stacked")
    q_stacked = sem("q_stacked")
    k_stacked = sem("k_stacked")
    totals_ready = sem("totals_ready")
    q_scaled = sem("q_scaled")
    k_scaled = sem("k_scaled")
    v_ready = sem("v_ready")
    chain = sem("la_chain")
    pool_chain = sem("la_pool_chain")
    passed = sem("la_passed")

    N_W = 10
    N_TOTALS = len(LEVELS) - 1
    block = ctx.enter_context(nc.Block())

    def blocks(ap, m):
        return ap.rearrange("p (n s m) -> p n s m", s=2, m=m)

    @block.sync
    def _(sp):
        sp.dma_start(w_in[:, :, :], ins["la_w_in"].rearrange("(c p) n -> p c n", p=P)).then_inc(weights_in, 16)
        sp.dma_start(w_comp[:, :, :], ins["la_w_comp"].rearrange("(c p) n -> p c n", p=P)).then_inc(weights_in, 16)
        sp.dma_start(w_v[:, :, :], ins["la_w_v"].rearrange("(c p) n -> p c n", p=P)).then_inc(weights_in, 16)
        sp.dma_start(w_y[:, :, :], ins["la_w_y"].rearrange("(c p) n -> p c n", p=P)).then_inc(weights_in, 16)
        sp.dma_start(w_out[:, :, :], ins["la_w_out"].rearrange("(c p) n -> p c n", p=P)).then_inc(weights_in, 16)
        sp.dma_start(h0[:, :, :], ins["la_h0"]).then_inc(weights_in, 16)
        sp.dma_start(bias_cols[:, :], ins["la_bias_cols"]).then_inc(weights_in, 16)
        sp.dma_start(v_bias[:, :], ins["la_v_bias"].to_broadcast([P, 2 * D])).then_inc(weights_in, 16)
        sp.dma_start(out_bias[:, :], ins["la_out_bias"].to_broadcast([P, D])).then_inc(weights_in, 16)
        sp.dma_start(level_masks[:, :, :], ins["la_masks"]).then_inc(weights_in, 16)

        def stack(dst, src, imaginary, done):
            src = src.rearrange("p (c t) -> p c t", c=KC)
            for j in range(4):
                rows = 64 * (j % 2) + 32 * imaginary
                sp.dma_start(dst[rows:rows + 32, j // 2:TILES:2, :], src[32 * j:32 * j + 32, :, :]).then_inc(done, 16)

        with sp.Fori(0, LA_ROUNDS) as r:
            sp.wait_ge(decay_ready, r + 1)
            for part in range(2):
                stack(total(1).rearrange("p (c t) -> p c t", c=TILES), decay[:, :], part, decay_stacked)
            sp.wait_ge(k_ready, r + 1)
            stack(k12, raw["kre"], 0, k_stacked)
            stack(k12, raw["kim"], 1, k_stacked)
            sp.wait_ge(q_ready, r + 1)
            stack(q12[:, 0], raw["qre"], 0, q_stacked)
            stack(q12[:, 1], raw["qre"], 1, q_stacked)
            stack(q12[:, 1], raw["qim"], 0, q_stacked)
            sp.wait_ge(negq_ready, r + 1)
            stack(q12[:, 0], neg_qim[:, :], 1, q_stacked)

    @block.tensor
    def _(pe):
        pe.wait_ge(weights_in, 16 * N_W)
        with pe.Fori(0, LA_ROUNDS) as r:
            def open_bank(use):
                n, before = banks.count(use, r)
                pe.wait_ge(banks.taken[n], before + 1)
                return banks.ps[n], banks.ready[n]

            def taken(use):
                n, before = banks.count(use, r)
                pe.wait_ge(banks.taken[n], before + 2)

            for c in range(KC):
                ps, ready = open_bank(("T", c))
                if c == 0:
                    pe.wait_ge(ln_done, r + 1)
                for g in range(G):
                    mm = pe.transpose(ps[:, g * T:(g + 1) * T], xhat[:, g, c * P:(c + 1) * P], ident[:, :])
                mm.then_inc(ready, 1)
            for m in range(KC):
                ps, ready = open_bank(("U", m))
                if m == 0:
                    taken(("T", 1))
                for c in range(KC):
                    mm = pe.matmul(ps[:, :], w_in[:, c, m * P:(m + 1) * P], xT[:, c, :], start=(c == 0), stop=(c == KC - 1))
                mm.then_inc(ready, 1)
            for n, comp in enumerate(COMPS):
                for m in range(KC):
                    ps, ready = open_bank((comp, m))
                    if n == 0 and m == 0:
                        taken(("U", KC - 1))
                    for c in range(KC):
                        mm = pe.matmul(ps[:, :], w_comp[:, c, n * D + m * P:n * D + (m + 1) * P], uT[:, c, :],
                                       start=(c == 0), stop=(c == KC - 1))
                    mm.then_inc(ready, 1)
            for g in range(G):
                ps, ready = open_bank(("V", g))
                for c in range(KC):
                    mm = pe.matmul(ps[:, :], uT[:, c, g * T:(g + 1) * T], w_v[:, c, :], start=(c == 0), stop=(c == KC - 1))
                mm.then_inc(ready, 1)

            pe.wait_ge(k_stacked, 16 * 8 * (r + 1))
            pe.wait_ge(q_stacked, 16 * 16 * (r + 1))
            for h in range(LA_HEADS):
                rows, c = slice(64 * (h % 2), 64 * (h % 2) + 64), h // 2
                for pair in range(2):
                    ps, ready = open_bank(("D", h, pair))
                    for n in range(2):
                        tok = slice((2 * pair + n) * T, (2 * pair + n + 1) * T)
                        mm = pe.matmul(ps[:, n * 2 * T:(n + 1) * 2 * T], k12[rows, c, tok], q12[rows, :, c, tok],
                                       start=True, stop=True)
                    mm.then_inc(ready, 1)
            for n, m in enumerate(LEVELS):
                for h in range(LA_HEADS):
                    rows, c = slice(64 * (h % 2), 64 * (h % 2) + 64), h // 2
                    ps, ready = open_bank(("S", m, h))
                    if h % 2 == 0:
                        pe.wait_ge(q_scaled, (TILES * (len(LEVELS) + 1)) * r + TILES * n + c + 1)
                        if n > 0:
                            pe.wait_ge(k_scaled, (TILES * (len(LEVELS) - 1)) * r + TILES * (n - 1) + c + 1)
                    for g in range(G):
                        tok = slice(g * T, (g + 1) * T)
                        right = q12[rows, :, c, tok].rearrange("p i (n s m) -> p i n s m", s=2, m=m)[:, :, :, 1, :]
                        mm = pe.matmul(ps[:, g * T:(g + 1) * T], k12[rows, c, tok], right, start=True, stop=True)
                    mm.then_inc(ready, 1)

            pe.wait_ge(q_scaled, (TILES * (len(LEVELS) + 1)) * (r + 1))
            taken(("S", LEVELS[MASK_LEVELS - 1], LA_HEADS - 1))
            for g in range(G):
                ps, ready = open_bank(("Y", g))
                if g == 0:
                    taken(("S", LEVELS[-1], LA_HEADS - 1))
                    pe.wait_ge(v_ready, G * (r + 1))
                tok = slice(g * T, (g + 1) * T)
                out = ps[:, :].rearrange("p (i h e) -> p i h e", i=2, h=LA_HEADS)
                for i in range(2):
                    for c in range(TILES):
                        pe.matmul(ps[:, i * D + c * 64:i * D + (c + 1) * 64], q12[:, i, c, tok], h0[:, c, :],
                                  start=(i == 0 and c == 0), stop=False, skip_group_check=True)
                for h in range(LA_HEADS):
                    for i in range(2):
                        at = LA_D * (1 - i)
                        mm = pe.matmul(out[:, :, h, :], s_all[:, h, g, i, :], v_sb[:, g, h, at:at + 2 * LA_D],
                                       start=False, stop=(h == LA_HEADS - 1 and i == 1), skip_group_check=True)
                mm.then_inc(ready, 1)
            for g in range(G):
                ps, ready = open_bank(("YT", g))
                taken(("Y", g))
                for c in range(2 * KC):
                    mm = pe.transpose(ps[:, c * T:(c + 1) * T], y_sb[:, g, c * P:(c + 1) * P], ident[:, :])
                mm.then_inc(ready, 1)
            for m in range(KC):
                ps, ready = open_bank(("Z", m))
                if m == 0:
                    taken(("YT", G - 1))
                for c in range(2 * KC):
                    mm = pe.matmul(ps[:, :], w_y[:, c, m * P:(m + 1) * P], yT[:, c, :], start=(c == 0), stop=(c == 2 * KC - 1))
                mm.then_inc(ready, 1)
            for g in range(G):
                ps, ready = open_bank(("O", g))
                if g == 0:
                    taken(("Z", KC - 1))
                for c in range(KC):
                    mm = pe.matmul(ps[:, 0:D], uT[:, c, g * T:(g + 1) * T], w_out[:, c, :], start=(c == 0), stop=(c == KC - 1))
                mm.then_inc(ready, 1)

    @block.scalar
    def _(act):
        act.wait_ge(weights_in, 16 * N_W)
        with act.Fori(0, LA_ROUNDS) as r:
            def take(use):
                n, before = banks.count(use, r)
                act.wait_ge(banks.ready[n], before + 1)
                return banks.ps[n], banks.taken[n]

            def gated(name, first):
                for m in range(KC):
                    ps, taken = take((name, m))
                    col = 2 * len(COMPS) + first + m
                    act.activation(uT[:, m, :], ps[:, :], ACT.Silu, bias=bias_cols[:, col:col + 1]).then_inc(taken, 1)

            for c in range(KC):
                ps, taken = take(("T", c))
                act.activation(xT[:, c, :], ps[:, :], ACT.Copy).then_inc(taken, 1)
            gated("U", 0)
            for n, comp in enumerate(COMPS):
                for m in range(KC):
                    ps, taken = take((comp, m))
                    act.activation(raw[comp][:, m * GT:(m + 1) * GT], ps[:, :], ACT.Identity,
                                   bias=bias_cols[:, KC * n + m:KC * n + m + 1]).then_inc(taken, 1)
            act.wait_ge(mag_ready, r + 1)
            act.activation(tmp[3], tmp[2], ACT.Sqrt).then_inc(root_ready, 1)
            act.wait_ge(q_ready, r + 1)
            act.activation(neg_qim[:, :], raw["qim"], ACT.Copy, scale=-1.0).then_inc(negq_ready, 1)
            for m in LEVELS[MASK_LEVELS:]:
                for h in range(LA_HEADS):
                    ps, taken = take(("S", m, h))
                    src = ps[:, :].rearrange("p (g i t) -> p g i t", g=G, i=2)
                    for b in range(T // (2 * m)):
                        rows = slice(2 * m * b, 2 * m * b + m)
                        last = act.activation(s_all[rows, h, :, :, 2 * m * b + m:2 * m * (b + 1)],
                                              src[rows, :, :, m * b:m * (b + 1)], ACT.Copy)
                    last.then_inc(taken, 1)
            for g in range(G):
                ps, taken = take(("Y", g))
                act.activation(y_sb[:, g, :], ps[:, :], ACT.Copy).then_inc(taken, 1)
            for g in range(G):
                ps, taken = take(("YT", g))
                act.activation(yT[:, :, g * T:(g + 1) * T], ps[:, :].rearrange("p (c t) -> p c t", c=2 * KC),
                               ACT.Copy).then_inc(taken, 1)
            gated("Z", KC)

    @block.gpsimd
    def _(pool):
        pool.wait_ge(weights_in, 16 * N_W)
        with pool.Fori(0, LA_ROUNDS) as r:
            xg = x_sb[:, bass.ds(r * G, G), :]
            pool.wait_ge(ln_done, r + 1)
            pool.tensor_tensor(xg, xg, out_bias[:, :].unsqueeze(1).to_broadcast([P, G, D]), ALU.add).then_inc(bias_added, 1)
            pool.wait_ge(decay_stacked, 16 * 8 * (r + 1))
            for n, m in enumerate(LEVELS[:-1]):
                pairs = total(m).rearrange("p (n s) -> p n s", s=2)
                if n > 0:
                    pool.wait_ge(totals_ready, N_TOTALS * r + n)
                pool.tensor_tensor(total(2 * m), pairs[:, :, 0], pairs[:, :, 1], ALU.mult).then_inc(totals_ready, 1)
            pool.wait_ge(totals_ready, N_TOTALS * (r + 1))
            for n, m in enumerate(LEVELS[:-1]):
                for c in range(TILES):
                    k, before = banks.count(("S", m, 2 * c + 1), r)
                    pool.wait_ge(banks.ready[k], before + 1)
                    left = blocks(k12[:, c, :], m)[:, :, 0, :]
                    nb = GT // (2 * m)
                    right_total = total(m).rearrange("p (c n s) -> p c n s", c=TILES, s=2)[:, c, :, 1]
                    pool.tensor_tensor(left, left, right_total.unsqueeze(2).to_broadcast([P, nb, m]),
                                       ALU.mult).then_inc(k_scaled, 1)

    @block.vector
    def _(dve):
        dve.wait_ge(weights_in, 16 * N_W)
        for n in range(8):
            dve.sem_inc(banks.taken[n], 1)
        links = [0]
        LINKS = 16 + 8 + 2 * len(LEVELS) + 2
        with dve.Fori(0, LA_ROUNDS) as r:
            def link(ins):
                links[0] += 1
                ins.then_inc(chain, 1)
                dve.wait_ge(chain, r * LINKS + links[0])

            def take(use):
                n, before = banks.count(use, r)
                dve.wait_ge(banks.ready[n], before + 1)
                return banks.ps[n], banks.taken[n]

            norm_group(dve, link, x_sb, r, xhat, ln_done, (stats, means, rstd, scratch, varc))

            n, before = banks.count(("aim", 1), r)
            dve.wait_ge(banks.taken[n], before + 2)
            mag2 = tmp[2]
            dve.tensor_tensor(tmp[0], raw["are"], raw["are"], ALU.mult)
            link(dve.tensor_tensor(tmp[1], raw["aim"], raw["aim"], ALU.mult))
            dve.tensor_tensor(mag2, tmp[0], tmp[1], ALU.add).then_inc(mag_ready, 1)
            dve.wait_ge(mag_ready, r + 1)
            link(dve.tensor_scalar(tmp[0], mag2, 1.0, None, ALU.add))
            link(dve.reciprocal(tmp[0], tmp[0]))
            dve.tensor_tensor(decay[:, :], mag2, tmp[0], ALU.mult).then_inc(decay_ready, 1)
            dve.wait_ge(root_ready, r + 1)
            dve.wait_ge(decay_ready, r + 1)
            link(dve.reciprocal(tmp[1], tmp[3]))
            link(dve.scalar_tensor_tensor(tmp[0], tmp[1], -0.5, tmp[1], ALU.mult, ALU.mult))
            link(dve.tensor_tensor(tmp[0], tmp[0], mag2, ALU.mult))
            link(dve.scalar_tensor_tensor(tmp[1], tmp[0], 1.5, tmp[1], ALU.add, ALU.mult))
            dve.tensor_tensor(raw["are"], raw["are"], tmp[1], ALU.mult)
            link(dve.tensor_tensor(raw["aim"], raw["aim"], tmp[1], ALU.mult))

            for m in LEVELS:
                nb = N2 // (2 * m)

                def carry(ap):
                    return blocks(ap, m)[:, :, 0, m - 1:m].to_broadcast([P, nb, m])

                def right(ap):
                    return blocks(ap, m)[:, :, 1, :]

                def part(n):
                    return tmp[n][:, 0:N2 // 2].rearrange("p (n m) -> p n m", m=m)
                dve.tensor_tensor(part(0), right(raw["are"]), carry(raw["are"]), ALU.mult)
                dve.tensor_tensor(part(1), right(raw["aim"]), carry(raw["aim"]), ALU.mult)
                dve.tensor_tensor(part(2), right(raw["are"]), carry(raw["aim"]), ALU.mult)
                link(dve.tensor_tensor(part(3), right(raw["aim"]), carry(raw["are"]), ALU.mult))
                dve.tensor_tensor(right(raw["are"]), part(0), part(1), ALU.subtract)
                link(dve.tensor_tensor(right(raw["aim"]), part(2), part(3), ALU.add))

            def turn_by_phase(re, im, sign, done):
                dve.tensor_tensor(tmp[0], raw[re], raw["are"], ALU.mult)
                dve.tensor_tensor(tmp[1], raw[im], raw["aim"], ALU.mult)
                dve.tensor_tensor(tmp[2], raw[im], raw["are"], ALU.mult)
                link(dve.tensor_tensor(tmp[3], raw[re], raw["aim"], ALU.mult))
                dve.tensor_tensor(raw[re], tmp[0], tmp[1], ALU.subtract if sign > 0 else ALU.add)
                dve.tensor_tensor(raw[im], tmp[2], tmp[3], ALU.add if sign > 0 else ALU.subtract).then_inc(done, 1)
                dve.wait_ge(done, r + 1)

            n, before = banks.count(("kim", 1), r)
            dve.wait_ge(banks.taken[n], before + 2)
            turn_by_phase("kre", "kim", -1, k_ready)
            n, before = banks.count(("qim", 1), r)
            dve.wait_ge(banks.taken[n], before + 2)
            turn_by_phase("qre", "qim", 1, q_ready)

            for g in range(G):
                ps, taken = take(("V", g))
                src = ps[:, :].rearrange("p (h e) -> p h e", h=LA_HEADS)
                bias = v_bias[:, :].rearrange("p (h e) -> p h e", h=LA_HEADS)
                dve.tensor_tensor(v_sb[:, g, :, LA_D:3 * LA_D], src, bias, ALU.add)
                dve.scalar_tensor_tensor(v_sb[:, g, :, 0:LA_D], src[:, :, LA_D:2 * LA_D], -1.0,
                                         bias[:, :, LA_D:2 * LA_D], ALU.mult, ALU.subtract).then_inc(v_ready, 1)
                dve.wait_ge(v_ready, G * r + g + 1)
                dve.sem_inc(taken, 1)

            def scale_queries(n, c):
                if n == 0:
                    if c == 0:
                        dve.wait_ge(decay_stacked, 16 * 8 * (r + 1))
                    take(("D", 2 * c + 1, 1))
                    q = q12[:, :, c, :]
                    one = total(1).rearrange("p (c t) -> p c t", c=TILES)[:, c, :]
                    dve.tensor_tensor(q, q, one.unsqueeze(1).to_broadcast([P, 2, GT]), ALU.mult).then_inc(q_scaled, 1)
                    return
                m = LEVELS[n - 1]
                nb = GT // (2 * m)
                if n == 1 and c == 0:
                    dve.wait_ge(totals_ready, N_TOTALS * (r + 1))
                take(("S", m, 2 * c + 1))
                for i in range(2):
                    q = blocks(q12[:, i, c, :], m)[:, :, 1, :]
                    left_total = total(m).rearrange("p (c n s) -> p c n s", c=TILES, s=2)[:, c, :, 0]
                    last = dve.tensor_tensor(q, q, left_total.unsqueeze(2).to_broadcast([P, nb, m]), ALU.mult)
                last.then_inc(q_scaled, 1)

            for c in range(TILES):
                for h in (2 * c, 2 * c + 1):
                    for pair in range(2):
                        ps, taken = take(("D", h, pair))
                        dst = s_all[:, h, 2 * pair:2 * pair + 2, :, :].rearrange("p g i t -> p (g i) t")
                        dve.tensor_tensor(dst, ps[:, :].rearrange("p (n t) -> p n t", n=4),
                                          ident[:, :].unsqueeze(1).to_broadcast([P, 4, T]), ALU.mult).then_inc(taken, 1)
                scale_queries(0, c)
            for n, m in enumerate(LEVELS):
                for c in range(TILES):
                    scale_queries(n + 1, c)
                    if n >= MASK_LEVELS:
                        continue
                    for h in (2 * c, 2 * c + 1):
                        ps, taken = take(("S", m, h))
                        dve.sem_inc(passed, 1)
                        dst = s_all[:, h].rearrange("p g i (n s m) -> p (g i) n s m", s=2, m=m)[:, :, :, 1, :]
                        mask = level_masks[:, n, :].rearrange("p (n m) -> p n m", m=m)
                        dve.copy_predicated(dst, mask.unsqueeze(1).to_broadcast([P, 2 * G, T // (2 * m), m]),
                                            ps[:, :].rearrange("p (a n m) -> p a n m", a=2 * G, m=m)).then_inc(taken, 1)
            dve.wait_ge(bias_added, r + 1)
            for g in range(G):
                xt = x_sb[:, r * G + g, :]
                ps, taken = take(("O", g))
                dve.tensor_tensor(xt, ps[:, 0:D], xt, ALU.add).then_inc(taken, 1)
        assert links[0] == LINKS, links[0]


EXPERTS, CAP = 8, B * T // 8
SLOTS = EXPERTS * CAP
CG = CAP // P


def experts(nc, ctx, x_sb, ins, consts, out):
    def sb(name, shape, dt=F32):
        return ctx.enter_context(nc.sbuf_tensor(name, shape, dt))

    def sem(name):
        return ctx.enter_context(nc.semaphore(name))

    ident = consts[0]
    slots_in = nc.dram_tensor("slots_in", [2 * SLOTS, D], F32, kind="Internal").ap()
    slots_out = nc.dram_tensor("slots_out", [SLOTS, D], F32, kind="Internal").ap()

    w1 = sb("ex_w1", [P, 2, KC, FF])
    w2 = sb("ex_w2", [P, 2, FC, D])
    w_r = sb("w_r", [P, KC, EXPERTS])
    before = sb("before", [P, P])
    ones = sb("ones", [P, P])
    countdown = sb("countdown", [P, EXPERTS])
    spill_row = sb("spill_row", [P, B])
    zeros = sb("zeros", [P, SLOTS * D // P // 8])
    xn = sb("xn", [P, B, D])
    xnT = sb("xnT", [P, KC, GT])
    xn_group = sb("xn_group", [P, G, D])
    small = [sb("ex_stats", [P, G, 6])] + [sb(f"ex_small{n}", [P, G, 1]) for n in range(4)]
    logits = sb("logits", [P, B, EXPERTS])
    top = sb("top", [P, B])
    expd = sb("ex_expd", [P, B, EXPERTS])
    hit = sb("hit", [P, B, EXPERTS])
    chosen = sb("chosen", [P, B, EXPERTS])
    first = sb("first", [P, B])
    run = [sb(f"run{n}", [P, B, EXPERTS]) for n in range(2)]
    rank = sb("rank", [P, B])
    keep = sb("keep", [P, B])
    weight = sb("weight", [P, B])
    slot = sb("slot", [P, B])
    spill = sb("spill", [P, B])
    slot_to = sb("slot_to", [P, B], I32)
    slot_from = sb("slot_from", [P, B], I32)
    rows = sb("ex_rows", [P, 2, CG, D])
    rowsT = sb("ex_rowsT", [P, 2, KC, CAP])
    hidT = sb("ex_hidT", [P, 2, FC, CAP])
    y_rows = sb("y_rows", [P, 2, CG, D])

    weights_in = sem("ex_weights_in")
    w_loaded = [sem(f"ex_w_loaded{n}") for n in range(2)]
    rows_loaded = [sem(f"ex_rows_loaded{n}") for n in range(2)]
    zeros_set = sem("zeros_set")
    zeroed = sem("zeroed")
    ln_done = sem("ex_ln_done")
    rT_ready = sem("rT_ready")
    rT_taken = sem("rT_taken")
    logit_ready = sem("logit_ready")
    logit_taken = sem("logit_taken")
    chosen_ready = sem("chosen_ready")
    ranks_ready = sem("ranks_ready")
    shifted_ready = sem("ex_shifted_ready")
    exp_ready = sem("ex_exp_ready")
    slots_ready = sem("slots_ready")
    scattered = sem("scattered")
    y_stored = [sem(f"y_stored{n}") for n in range(2)]
    gathered = [sem(f"gathered{n}") for n in range(GATHERS)]
    combined = sem("combined")
    stored = sem("stored")
    chain = sem("ex_chain")

    uses = []
    for par in range(2):
        uses += [("T", par, c) for c in range(KC)] + [("F1", par, f) for f in range(FC)] + [("F2", par, t) for t in range(CG)]
    banks = Banks(nc, ctx, "ex", uses, n=5)
    ps_T = [ctx.enter_context(nc.psum_tensor(f"ps_rT{n}", [P, 512], F32)) for n in range(KC)]
    ps_r = ctx.enter_context(nc.psum_tensor("ps_r", [P, 512], F32))

    N_W = 5
    ROUNDS = B // G
    block = ctx.enter_context(nc.Block())

    @block.sync
    def _(sp):
        sp.dma_start(w_r[:, :, :], ins["ex_w_r"].rearrange("(c p) n -> p c n", p=P)).then_inc(weights_in, 16)
        sp.dma_start(before[:, :], ins["before"]).then_inc(weights_in, 16)
        sp.dma_start(ones[:, :], ins["ones"]).then_inc(weights_in, 16)
        sp.dma_start(countdown[:, :], ins["countdown"].to_broadcast([P, EXPERTS])).then_inc(weights_in, 16)
        sp.dma_start(spill_row[:, :], ins["spill_row"]).then_inc(weights_in, 16)

        def load_weights(e, par):
            sp.dma_start(w1[:, par], ins["ex_w1"][bass.ds(e, 1)].rearrange("a (c p) n -> p (a c) n", p=P)
                         ).then_inc(w_loaded[par], 16)
            sp.dma_start(w2[:, par], ins["ex_w2"][bass.ds(e, 1)].rearrange("a (c p) n -> p (a c) n", p=P)
                         ).then_inc(w_loaded[par], 16)

        def load_rows(e, par):
            sp.dma_start(rows[:, par], slots_in[bass.ds(e * CAP, CAP), :].rearrange("(t p) d -> p t d", p=P)
                         ).then_inc(rows_loaded[par], 16)

        load_weights(0, 0)
        load_weights(1, 1)
        sp.wait_ge(zeros_set, 1)
        for n in range(8):
            at = n * SLOTS // 8
            sp.dma_start(slots_in[at:at + SLOTS // 8, :].rearrange("(p a) d -> p (a d)", p=P), zeros[:, :]).then_inc(zeroed, 16)
        sp.wait_ge(scattered, 16 * B)
        load_rows(0, 0)
        load_rows(1, 1)

        def store(r, par):
            n, before_ = banks.count(("F2", par, CG - 1), r)
            sp.wait_ge(banks.taken[n], before_ + 2)
            sp.dma_start(slots_out[bass.ds((2 * r + par) * CAP, CAP), :].rearrange("(t p) d -> p t d", p=P),
                         y_rows[:, par]).then_inc(y_stored[par], 16)

        with sp.Fori(0, EXPERTS // 2 - 1) as r:
            for par in range(2):
                store(r, par)
                load_weights(2 * r + 2 + par, par)
                load_rows(2 * r + 2 + par, par)
        for par in range(2):
            store(EXPERTS // 2 - 1, par)
        for g in range(B // G):
            sp.wait_ge(combined, G * (g + 1))
            sp.dma_start(out[g * G:(g + 1) * G].rearrange("b t d -> t b d"), x_sb[:, g * G:(g + 1) * G, :]).then_inc(stored, 16)
        sp.wait_ge(stored, 16 * (B // G))

    @block.gpsimd
    def _(pool):
        pool.memset(zeros[:, :], 0.0).then_inc(zeros_set, 1)
        pool.wait_ge(zeroed, 16 * 8)
        pool.wait_ge(slots_ready, 1)
        for b in range(B):
            pool.indirect_dma_start(out=slots_in[:, :], out_offset=bass.IndirectOffsetOnAxis(ap=slot_to[:, b:b + 1], axis=0),
                                    in_=xn[:, b, :], in_offset=None).then_inc(scattered, 16)
        for par in range(2):
            pool.wait_ge(y_stored[par], 16 * (EXPERTS // 2 + 1))
        pool.wait_ge(scattered, 16 * B)
        for b in range(B):
            if b >= GATHERS:
                pool.wait_ge(combined, b - GATHERS + 1)
            pool.indirect_dma_start(out=xn[:, b, :], out_offset=None, in_=slots_out[:, :],
                                    in_offset=bass.IndirectOffsetOnAxis(ap=slot_from[:, b:b + 1], axis=0)
                                    ).then_inc(gathered[b % GATHERS], 16)

    @block.tensor
    def _(pe):
        pe.wait_ge(weights_in, 16 * N_W)
        with pe.Fori(0, ROUNDS) as r:
            pe.wait_ge(logit_taken, r + 1)
            pe.wait_ge(ln_done, r + 1)
            for c in range(KC):
                for g in range(G):
                    mm = pe.transpose(ps_T[c][:, g * T:(g + 1) * T], xn_group[:, g, c * P:(c + 1) * P], ident[:, :])
            mm.then_inc(rT_ready, 1)
            pe.wait_ge(rT_taken, r + 1)
            for g in range(G):
                for c in range(KC):
                    mm = pe.matmul(ps_r[:, g * EXPERTS:(g + 1) * EXPERTS], xnT[:, c, g * T:(g + 1) * T], w_r[:, c, :],
                                   start=(c == 0), stop=(c == KC - 1))
            mm.then_inc(logit_ready, 1)
        pe.wait_ge(chosen_ready, 1)
        flat = chosen[:, :, :].rearrange("p b e -> p (b e)")
        pe.matmul(ps_T[0][:, 0:B * EXPERTS], before[:, :], flat, start=True, stop=True)
        pe.matmul(ps_T[1][:, 0:B * EXPERTS], ones[:, :], flat, start=True, stop=True).then_inc(ranks_ready, 1)

        with pe.Fori(0, EXPERTS // 2) as r:
            def open_bank(use):
                n, before_ = banks.count(use, r)
                pe.wait_ge(banks.taken[n], before_ + 1)
                return banks.ps[n], banks.ready[n]

            def taken(use):
                n, before_ = banks.count(use, r)
                pe.wait_ge(banks.taken[n], before_ + 2)

            for par in range(2):
                pe.wait_ge(rows_loaded[par], 16 * (r + 1))
                for c in range(KC):
                    ps, ready = open_bank(("T", par, c))
                    for t in range(CG):
                        mm = pe.transpose(ps[:, t * P:(t + 1) * P], rows[:, par, t, c * P:(c + 1) * P], ident[:, :])
                    mm.then_inc(ready, 1)
                pe.wait_ge(w_loaded[par], 32 * (r + 1))
                for f in range(FC):
                    ps, ready = open_bank(("F1", par, f))
                    if f == 0:
                        taken(("T", par, KC - 1))
                    for c in range(KC):
                        mm = pe.matmul(ps[:, :], w1[:, par, c, f * P:(f + 1) * P], rowsT[:, par, c, :],
                                       start=(c == 0), stop=(c == KC - 1))
                    mm.then_inc(ready, 1)
                for t in range(CG):
                    ps, ready = open_bank(("F2", par, t))
                    if t == 0:
                        taken(("F1", par, FC - 1))
                    for f in range(FC):
                        mm = pe.matmul(ps[:, 0:D], hidT[:, par, f, t * P:(t + 1) * P], w2[:, par, f, :],
                                       start=(f == 0), stop=(f == FC - 1))
                    mm.then_inc(ready, 1)

    @block.scalar
    def _(act):
        with act.Fori(0, ROUNDS) as r:
            act.wait_ge(rT_ready, r + 1)
            for c in range(KC):
                last = act.activation(xnT[:, c, :], ps_T[c][:, :], ACT.Copy)
            last.then_inc(rT_taken, 1)
        act.wait_ge(shifted_ready, 1)
        act.activation(expd[:, :, :], expd[:, :, :], ACT.Exp).then_inc(exp_ready, 1)
        with act.Fori(0, EXPERTS // 2) as r:
            def take(use):
                n, before_ = banks.count(use, r)
                act.wait_ge(banks.ready[n], before_ + 1)
                return banks.ps[n], banks.taken[n]

            for par in range(2):
                for c in range(KC):
                    ps, taken = take(("T", par, c))
                    act.activation(rowsT[:, par, c, :], ps[:, :], ACT.Copy).then_inc(taken, 1)
                for f in range(FC):
                    ps, taken = take(("F1", par, f))
                    act.activation(hidT[:, par, f, :], ps[:, :], ACT.Relu).then_inc(taken, 1)

    @block.vector
    def _(dve):
        dve.wait_ge(weights_in, 16 * N_W)
        for n in range(banks.n):
            dve.sem_inc(banks.taken[n], 1)
        dve.sem_inc(logit_taken, 1)
        for par in range(2):
            dve.sem_inc(y_stored[par], 16)
        links = [0]
        base = [0]

        def link(ins):
            links[0] += 1
            ins.then_inc(chain, 1)
            dve.wait_ge(chain, base[0] + links[0])

        with dve.Fori(0, ROUNDS) as r:
            base[0] = r * 16
            norm_group(dve, link, x_sb, r, xn_group, ln_done, small)
            dve.wait_ge(ln_done, r + 1)
            dve.tensor_copy(xn[:, bass.ds(r * G, G), :], xn_group[:, :, :])
            dve.wait_ge(logit_ready, r + 1)
            dve.tensor_copy(logits[:, bass.ds(r * G, G), :].rearrange("p b e -> p (b e)"),
                            ps_r[:, 0:G * EXPERTS]).then_inc(logit_taken, 1)
        assert links[0] == 16
        base[0], links[0] = 16 * ROUNDS, 0
        dve.wait_ge(logit_taken, ROUNDS + 1)

        def wide(ap):
            return ap.unsqueeze(2).to_broadcast([P, B, EXPERTS])

        order = countdown[:, :].unsqueeze(1).to_broadcast([P, B, EXPERTS])
        link(dve.tensor_reduce(top[:, :], logits[:, :, :], AX.X, ALU.max))
        dve.tensor_tensor(expd[:, :, :], logits[:, :, :], wide(top[:, :]), ALU.subtract).then_inc(shifted_ready, 1)
        link(dve.tensor_tensor(hit[:, :, :], logits[:, :, :], wide(top[:, :]), ALU.is_equal))
        link(dve.tensor_tensor(hit[:, :, :], hit[:, :, :], order, ALU.mult))
        link(dve.tensor_reduce(first[:, :], hit[:, :, :], AX.X, ALU.max))
        dve.tensor_tensor(chosen[:, :, :], order, wide(first[:, :]), ALU.is_equal).then_inc(chosen_ready, 1)
        dve.wait_ge(exp_ready, 1)
        link(dve.tensor_reduce(weight[:, :], expd[:, :, :], AX.X, ALU.add))
        link(dve.reciprocal(weight[:, :], weight[:, :]))
        dve.wait_ge(ranks_ready, 1)
        totals = ps_T[1][:, 0:B * EXPERTS].rearrange("p (b e) -> p b e", e=EXPERTS)
        dve.memset(run[0][:, 0:1, :], 0.0)
        link(dve.tensor_copy(run[0][:, 1:B, :], totals[:, 0:B - 1, :]))
        step, cur = 1, 0
        while step < B:
            dve.tensor_copy(run[1 - cur][:, 0:step, :], run[cur][:, 0:step, :])
            link(dve.tensor_tensor(run[1 - cur][:, step:B, :], run[cur][:, step:B, :], run[cur][:, 0:B - step, :], ALU.add))
            step, cur = 2 * step, 1 - cur
        within = ps_T[0][:, 0:B * EXPERTS].rearrange("p (b e) -> p b e", e=EXPERTS)
        link(dve.tensor_tensor(hit[:, :, :], within, run[cur][:, :, :], ALU.add))
        link(dve.tensor_tensor(hit[:, :, :], hit[:, :, :], chosen[:, :, :], ALU.mult))
        link(dve.tensor_reduce(rank[:, :], hit[:, :, :], AX.X, ALU.add))
        dve.tensor_scalar(keep[:, :], rank[:, :], float(CAP), None, ALU.is_lt)
        link(dve.scalar_tensor_tensor(slot[:, :], first[:, :], -float(CAP), rank[:, :], ALU.mult, ALU.add))
        link(dve.tensor_scalar(slot[:, :], slot[:, :], float(SLOTS), None, ALU.add))
        link(dve.tensor_tensor(spill[:, :], slot[:, :], spill_row[:, :], ALU.subtract))
        link(dve.tensor_tensor(spill[:, :], spill[:, :], keep[:, :], ALU.mult))
        dve.tensor_tensor(slot_to[:, :], spill[:, :], spill_row[:, :], ALU.add)
        dve.tensor_tensor(weight[:, :], weight[:, :], keep[:, :], ALU.mult)
        dve.tensor_tensor(slot_from[:, :], slot[:, :], keep[:, :], ALU.mult).then_inc(slots_ready, 1)

        with dve.Fori(0, EXPERTS // 2) as r:
            for par in range(2):
                for t in range(CG):
                    n, before_ = banks.count(("F2", par, t), r)
                    dve.wait_ge(banks.ready[n], before_ + 1)
                    if t == 0:
                        dve.wait_ge(y_stored[par], 16 * (r + 1))
                    dve.tensor_copy(y_rows[:, par, t, :], banks.ps[n][:, 0:D]).then_inc(banks.taken[n], 1)
        for b in range(B):
            dve.wait_ge(gathered[b % GATHERS], 16 * (b // GATHERS + 1))
            dve.scalar_tensor_tensor(x_sb[:, b, :], xn[:, b, :], weight[:, b:b + 1], x_sb[:, b, :], ALU.mult,
                                     ALU.add).then_inc(combined, 1)


def program(nc, ins, outs):
    with ExitStack() as ctx:
        def sb(name, shape, dt=F32):
            return ctx.enter_context(nc.sbuf_tensor(name, shape, dt))

        x_sb = sb("x_sb", [P, B, D])
        ident = sb("ident", [P, P])
        ident16 = sb("ident16", [P, P], BF16)
        causal = sb("causal", [P, 4, T], BF16)
        half_masks = sb("half_masks", [P, 2])
        with ExitStack() as part:
            transformer(nc, part, x_sb, ins, (ident, ident16, causal, half_masks))
        with ExitStack() as part:
            linear_attention(nc, part, x_sb, ins, (ident,))
        with ExitStack() as part:
            experts(nc, part, x_sb, ins, (ident,), outs[0])


_OUTS = [((B, T, D), "float32")]


def lay_out(inputs):
    import numpy as np

    def tok(name):
        return np.ascontiguousarray(inputs["L0_tok_" + name])

    def cols(a):
        return a.reshape(a.shape[0], -1, P).transpose(0, 2, 1)

    a = {"idxT": np.asarray(inputs["x"]).T, "tok_emb": tok("tok_emb"), "pos_emb": tok("pos_emb")}
    for name in ("wq", "wk", "wv", "w_proj", "w1", "w2", "b_proj", "b2"):
        a[name] = tok(name)
    a["b1_cols"] = cols(tok("b1"))
    a["ln1_cols"] = np.concatenate([cols(tok("ln1_w")), cols(tok("ln1_b"))], axis=2)
    a["ln2_cols"] = np.concatenate([cols(tok("ln2_w")), cols(tok("ln2_b"))], axis=2)
    row = np.arange(P)
    a["ident"] = np.eye(P, dtype=np.float32)
    a["causal"] = np.where(row[None, :] > row[:, None], MASKED, 0.0).astype(np.float32)
    even = (row % (2 * HD) < HD)
    a["half_masks"] = np.stack([even, ~even], axis=1).astype(np.float32)

    def la(name):
        return np.asarray(inputs["L0_attn_" + name])

    a["la_w_in"] = la("W_in").T
    parts = la("W_qkva").reshape(D, 4, 2, D)
    bias = la("b_qkva").reshape(D, 4, 2)
    at = {"q": 0, "k": 1, "v": 2, "a": 3, "re": 0, "im": 1}
    a["la_w_comp"] = np.concatenate([parts[:, at[c[0]], at[c[1:]], :].T for c in COMPS], axis=1)
    v_rows = parts[:, 2].reshape(LA_HEADS, LA_D, 2, D).transpose(3, 0, 2, 1)
    a["la_w_v"] = v_rows.reshape(D, 2 * D)
    a["la_v_bias"] = bias[:, 2].reshape(LA_HEADS, LA_D, 2).transpose(0, 2, 1).reshape(1, 2 * D)
    a["la_w_y"] = la("W_y").reshape(D, LA_HEADS, LA_D, 2).transpose(3, 1, 2, 0).reshape(2 * D, D)
    a["la_w_out"] = la("W_out").T
    a["la_out_bias"] = la("b_out").reshape(1, D)
    columns = [bias[:, at[c[0]], at[c[1:]]] for c in COMPS] + [la("b_in"), la("b_y")]
    a["la_bias_cols"] = np.concatenate([c.reshape(KC, P).T for c in columns], axis=1)
    h0 = np.zeros((TILES, 2, 2, LA_D, 2, LA_D), np.float32)
    for n, name in enumerate(("h0_re", "h0_im")):
        for h in range(LA_HEADS):
            h0[h // 2, h % 2, n, :, h % 2, :] = la(name)[h]
    a["la_h0"] = h0.reshape(TILES, P, 2 * LA_D).transpose(1, 0, 2)
    masks = np.zeros((P, MASK_LEVELS, T // 2), np.uint32)
    for n, m in enumerate(LEVELS[:MASK_LEVELS]):
        for j in range(T // 2):
            block = j // m
            masks[2 * m * block:2 * m * block + m, n, j] = 1
    a["la_masks"] = masks

    a["ex_w_r"] = np.asarray(inputs["L0_ffn_Wr"])
    a["ex_w1"] = np.asarray(inputs["L0_ffn_W1"])
    a["ex_w2"] = np.asarray(inputs["L0_ffn_W2"])
    a["before"] = (row[:, None] < row[None, :]).astype(np.float32)
    a["ones"] = np.ones((P, P), np.float32)
    a["countdown"] = np.arange(EXPERTS, 0, -1, dtype=np.float32)[None]
    a["spill_row"] = (SLOTS + T * np.arange(B)[None, :] + row[:, None]).astype(np.float32)
    return {k: np.ascontiguousarray(v) for k, v in a.items()}


def kernel(**inputs):
    import numpy as _np
    import concourse.bacc as _bacc
    from concourse import mybir as _mybir
    from concourse.bass_utils import run_bass_kernel_spmd as _run

    nc = _bacc.Bacc("TRN2", target_bir_lowering=False, num_devices=1)
    arrays, ins = {}, {}
    for name, a in lay_out(inputs).items():
        arrays[f"in_{name}_dram"] = a
        ins[name] = nc.dram_tensor(f"in_{name}_dram", a.shape, _mybir.dt.from_np(a.dtype), kind="ExternalInput").ap()
    outs = [nc.dram_tensor(f"out_{i}_dram", shape, _mybir.dt.from_np(_np.dtype(dtype)), kind="ExternalOutput").ap()
            for i, (shape, dtype) in enumerate(_OUTS)]
    program(nc, ins, outs)
    r = _run(nc, [arrays], core_ids=[0])
    return r.results[0]["out_0_dram"]
```

```python
from contextlib import ExitStack

import concourse.bass as bass
from concourse import mybir

F32 = mybir.dt.float32
I32 = mybir.dt.int32
U32 = mybir.dt.uint32
ALU = mybir.AluOpType
ACT = mybir.ActivationFunctionType
AX = mybir.AxisListType

P = 128
B, T, D = 32, 128, 256
KC = D // P
LAYERS, HEADS = 4, 16
HD = D // HEADS
HV = HD + 1
FF = 4 * D
FC = FF // P
G = 4
STEPS_L = B // G
STEPS = LAYERS * STEPS_L
GT = G * T
UNITS = 4 * G
EPS = 1e-5
MASKED = -1e30
RSQRT_MAGIC = 0x5F3759DF


def at_least(eng, sem, value):
    if isinstance(value, int) and value <= 0:
        return
    eng.wait_ge(sem, value)


class Step:

    def __init__(self, kind, i):
        self.kind, self.i = kind, i


def step_uses(kind):
    uses = [("T1", 0), ("T1", 1), ("Q", 0), ("Q", 1), ("K", 0), ("K", 1), ("V", 0), ("V", 1), ("T2", 0), ("T2", 1)]
    for u in range(UNITS):
        if u < FC:
            uses.append(("F1", u))
        elif u % 2 == 0 and u < UNITS - 2:
            uses.append(("F2", (u - FC) // 2))
        if u >= 6 and u % 4 == 2:
            uses.append(("CT", (u - 6) // 4))
        if u >= 7 and u % 4 == 3:
            uses.append(("PJ", (u - 7) // 4))
    uses += [("F2", G - 1), ("CT", G - 1), ("PJ", G - 1)]
    attn = ("T1", "Q", "K", "V", "CT", "PJ")
    return [u if kind == "body" or (u[0] in attn) == (kind == "first") else None for u in uses]


NBANK = 3
GATHERS = 4


def bank_of(step, name, idx):
    uses = step_uses(step.kind)
    at = uses.index((name, idx))
    bank = at % NBANK
    before = sum(1 for n in range(bank, at, NBANK) if uses[n] is not None)
    if step.kind == "first":
        return bank, before
    firsts = sum(1 for n in range(bank, len(uses), NBANK) if step_uses("first")[n] is not None)
    per = len(uses) // NBANK
    assert len(uses) % NBANK == 0
    return bank, firsts + (step.i - 1) * per + before


def norm_group(dve, link, x_sb, g, dst, done, small):
    norm_stats(dve, link, x_sb, g, small)
    norm_scale(dve, link, small)
    norm_apply(dve, x_sb, g, dst, done, small)


def norm_stats(dve, link, x_sb, g, small):
    for t in range(G):
        last = dve.bn_stats(small[0][:, t, :], x_sb[:, g * G + t, :])
    link(last)


def norm_scale(dve, link, small):
    stats, means, rstd, scratch, varc = small
    rs, sc, va, mean = rstd[:, :, 0], scratch[:, :, 0], varc[:, :, 0], means[:, :, 0]
    dve.tensor_tensor(mean, stats[:, :, 1], stats[:, :, 4], ALU.add)
    dve.tensor_tensor(sc, stats[:, :, 1], stats[:, :, 4], ALU.subtract)
    link(dve.tensor_tensor(va, stats[:, :, 2], stats[:, :, 5], ALU.add))
    dve.tensor_scalar(mean, mean, 0.5, None, ALU.mult)
    link(dve.scalar_tensor_tensor(sc, sc, 0.25, sc, ALU.mult, ALU.mult))
    link(dve.scalar_tensor_tensor(va, va, 1.0 / D, sc, ALU.mult, ALU.add))
    link(dve.tensor_scalar(va, va, EPS, None, ALU.add))
    link(dve.tensor_scalar(sc.bitcast(I32), va.bitcast(I32), 1, None, ALU.logical_shift_right))
    link(dve.tensor_scalar(rs.bitcast(I32), sc.bitcast(I32), -1.0, float(RSQRT_MAGIC), ALU.mult, ALU.add))
    for _ in range(3):
        link(dve.scalar_tensor_tensor(sc, rs, -0.5, rs, ALU.mult, ALU.mult))
        link(dve.tensor_tensor(sc, sc, va, ALU.mult))
        link(dve.scalar_tensor_tensor(rs, sc, 1.5, rs, ALU.add, ALU.mult))


def norm_apply(dve, x_sb, g, dst, done, small):
    stats, means, rstd, scratch, varc = small
    for t in range(G):
        last = dve.tensor_scalar(dst[:, t, :], x_sb[:, g * G + t, :], means[:, t, :], rstd[:, t, :],
                                 ALU.subtract, ALU.mult)
    last.then_inc(done, 1)


def transformer(nc, ctx, x_sb, ins, consts):
    def sb(name, shape, dt=F32):
        return ctx.enter_context(nc.sbuf_tensor(name, shape, dt))

    def sem(name):
        return ctx.enter_context(nc.semaphore(name))

    ident, causal, head_masks = consts

    wqkv = sb("wqkv", [P, KC, 3 * D])
    wproj = sb("wproj", [P, KC, D])
    w1 = sb("w1", [P, KC, FF])
    w2 = sb("w2", [P, FC, D])
    ln1 = sb("ln1", [P, 2 * KC])
    ln2 = sb("ln2", [P, 2 * KC])
    b1 = sb("b1", [P, FC])
    bproj = sb("bproj", [P, D])
    b2 = sb("b2", [P, D])

    idx = sb("idx", [P, B], I32)
    pos = sb("pos", [P, D])
    xhat1 = sb("xhat1", [P, G, D])
    xhat2 = sb("xhat2", [P, G, D])
    stats = sb("stats", [P, G, 6])
    means = sb("means", [P, G, 1])
    rstd = sb("rstd", [P, G, 1])
    scratch = sb("scratch", [P, G, 1])
    varc = sb("varc", [P, G, 1])
    x1T = sb("x1T", [P, KC, GT])
    x2T = sb("x2T", [P, KC, GT])
    qT = sb("qT", [P, KC, GT])
    kT = sb("kT", [P, KC, 4, GT])
    v1 = sb("v1", [P, G, HEADS, HV])
    rowmax = sb("rowmax", [P, 3, 4])
    shifted = sb("shifted", [P, 3, 4 * T])
    probs = sb("probs", [P, 2, 4 * T])
    probsT = sb("probsT", [P, 2, 4 * T])
    rsum = sb("rsum", [P, HEADS])
    ctx_sb = sb("ctx_sb", [P, 2, D])
    ctxT = sb("ctxT", [P, 2, KC, T])
    hidT = sb("hidT", [P, FC, GT])

    def bank(name):
        return ctx.enter_context(nc.psum_tensor(name, [P, 512], F32))

    ps_scores = [bank(f"ps_scores{n}") for n in range(2)]
    ps_probsT = [bank(f"ps_probsT{n}") for n in range(2)]
    ps_ctx = bank("ps_ctx")
    ps_mm = [bank(f"ps_mm{n}") for n in range(NBANK)]

    consts_in = sem("consts_in")
    idx_in = sem("idx_in")
    rows_in = [sem(f"rows_in{n}") for n in range(GATHERS)]
    embedded = sem("embedded")
    attn_w_in = sem("attn_w_in")
    ffn_w_in = sem("ffn_w_in")
    mm_ready = [sem(f"mm_ready{n}") for n in range(NBANK)]
    mm_taken = [sem(f"mm_taken{n}") for n in range(NBANK)]
    ones_set = sem("ones_set")
    ln1_done = sem("ln1_done")
    ln2_done = sem("ln2_done")
    bproj_added = sem("bproj_added")
    b2_added = sem("b2_added")
    scores_ready = sem("scores_ready")
    scores_taken = sem("scores_taken")
    shifted_ready = sem("shifted_ready")
    probs_ready = sem("probs_ready")
    probsT_ready = sem("probsT_ready")
    probsT_taken = sem("probsT_taken")
    pv_done = sem("pv_done")
    ctx_taken = sem("ctx_taken")
    dve_chain = sem("dve_chain")

    N_ATTN_W, N_FFN_W, N_CONST = 6, 5, 3
    x_tok = ins["tok_emb"]
    block = ctx.enter_context(nc.Block())

    def layer_of(i):
        return i // STEPS_L

    def group(i):
        return i % STEPS_L

    @block.sync
    def _(sp):
        sp.dma_start(idx[:, :], ins["idxT"]).then_inc(idx_in, 16)
        sp.dma_start(pos[:, :], ins["pos_emb"][0:T, :]).then_inc(idx_in, 16)
        sp.dma_start(ident[:, :], ins["ident"]).then_inc(consts_in, 16)
        sp.dma_start(causal[:, :], ins["causal"]).then_inc(consts_in, 16)
        sp.dma_start(head_masks[:, :], ins["head_masks"]).then_inc(consts_in, 16)

        def row_bcast(name, l):
            return ins[name][bass.ds(l, 1), :].to_broadcast([P, D])

        def load_attn(l):
            for n, w in enumerate(("wq", "wk", "wv")):
                sp.dma_start(wqkv[:, :, n * D:(n + 1) * D],
                             ins[w][bass.ds(l, 1)].rearrange("a (c p) n -> p (a c) n", p=P)).then_inc(attn_w_in, 16)
            sp.dma_start(wproj[:, :, :],
                         ins["w_proj"][bass.ds(l, 1)].rearrange("a (c p) n -> p (a c) n", p=P)).then_inc(attn_w_in, 16)
            sp.dma_start(ln1[:, :], ins["ln1_cols"][bass.ds(l, 1)].rearrange("a p n -> (a p) n")).then_inc(attn_w_in, 16)
            sp.dma_start(bproj[:, :], row_bcast("b_proj", l)).then_inc(attn_w_in, 16)

        def load_ffn(l):
            sp.dma_start(ln2[:, :], ins["ln2_cols"][bass.ds(l, 1)].rearrange("a p n -> (a p) n")).then_inc(ffn_w_in, 16)
            sp.dma_start(w1[:, :, :],
                         ins["w1"][bass.ds(l, 1)].rearrange("a (c p) n -> p (a c) n", p=P)).then_inc(ffn_w_in, 16)
            sp.dma_start(w2[:, :, :],
                         ins["w2"][bass.ds(l, 1)].rearrange("a (c p) n -> p (a c) n", p=P)).then_inc(ffn_w_in, 16)
            sp.dma_start(b1[:, :], ins["b1_cols"][bass.ds(l, 1)].rearrange("a p n -> (a p) n")).then_inc(ffn_w_in, 16)
            sp.dma_start(b2[:, :], row_bcast("b2", l)).then_inc(ffn_w_in, 16)

        load_attn(0)
        load_ffn(0)
        with sp.Fori(1, LAYERS) as l:
            n, before = bank_of(Step("body", l * STEPS_L - 1), "PJ", G - 1)
            sp.wait_ge(mm_ready[n], before + 1)
            sp.wait_ge(bproj_added, l * STEPS_L)
            load_attn(l)
            n, before = bank_of(Step("body", l * STEPS_L), "F2", G - 1)
            sp.wait_ge(mm_ready[n], before + 1)
            sp.wait_ge(b2_added, l * STEPS_L)
            load_ffn(l)

    @block.gpsimd
    def _(pool):
        pool.memset(v1[:, :, :, HD:HV].rearrange("p g h o -> p (g h) o"), 1.0).then_inc(ones_set, 1)
        pool.wait_ge(idx_in, 32)

        def gather(b, n):
            pool.indirect_dma_start(out=x_sb[:, b, :], out_offset=None, in_=x_tok[:, :],
                                    in_offset=bass.IndirectOffsetOnAxis(ap=idx[:, b:b + 1], axis=0)
                                    ).then_inc(rows_in[n], 16)

        def add_pos(b, n):
            pool.wait_ge(rows_in[n], 16 * (b // GATHERS + 1))
            pool.tensor_tensor(x_sb[:, b, :], x_sb[:, b, :], pos[:, :], ALU.add).then_inc(embedded, 1)

        for b in range(GATHERS):
            gather(b, b)
        for b in range(B):
            add_pos(b, b % GATHERS)
            if b + GATHERS < B:
                gather(b + GATHERS, b % GATHERS)

        def bproj_add(i):
            xg = x_sb[:, bass.ds(group(i) * G, G), :]
            pool.wait_ge(attn_w_in, 16 * N_ATTN_W * (layer_of(i) + 1))
            pool.wait_ge(ln1_done, i + 1)
            pool.tensor_tensor(xg, xg, bproj[:, :].unsqueeze(1).to_broadcast([P, G, D]), ALU.add).then_inc(bproj_added, 1)

        def b2_add(i):
            xg = x_sb[:, bass.ds(group(i) * G, G), :]
            pool.wait_ge(ffn_w_in, 16 * N_FFN_W * (layer_of(i) + 1))
            pool.wait_ge(ln2_done, i + 1)
            pool.tensor_tensor(xg, xg, b2[:, :].unsqueeze(1).to_broadcast([P, G, D]), ALU.add).then_inc(b2_added, 1)

        bproj_add(0)
        with pool.Fori(1, STEPS) as i:
            b2_add(i - 1)
            bproj_add(i)
        b2_add(STEPS - 1)

    @block.tensor
    def _(pe):
        def open_bank(step, name, idx):
            n, before = bank_of(step, name, idx)
            at_least(pe, mm_taken[n], before)
            return ps_mm[n], mm_ready[n]

        def turn(step, name, src, done):
            for c in range(KC):
                ps, ready = open_bank(step, name, c)
                if c == 0:
                    pe.wait_ge(*done)
                for t in range(G):
                    mm = pe.transpose(ps[:, t * T:(t + 1) * T], src[:, t, c * P:(c + 1) * P], ident[:, :])
                mm.then_inc(ready, 1)

        def taken(step, name, idx):
            n, before = bank_of(step, name, idx)
            pe.wait_ge(mm_taken[n], before + 1)

        def qkv(step):
            i = step.i
            pe.wait_ge(attn_w_in, 16 * N_ATTN_W * (layer_of(i) + 1))
            taken(step, "T1", 0)
            for w, name in enumerate(("Q", "K")):
                for m in range(KC):
                    ps, ready = open_bank(step, name, m)
                    for c in range(KC):
                        if (w, m, c) == (0, 0, 1):
                            taken(step, "T1", 1)
                        mm = pe.matmul(ps[:, :], wqkv[:, c, w * D + m * P:w * D + (m + 1) * P], x1T[:, c, :],
                                       start=(c == 0), stop=(c == KC - 1))
                    mm.then_inc(ready, 1)
            for n in range(2):
                ps, ready = open_bank(step, "V", n)
                for t in range(2):
                    for c in range(KC):
                        mm = pe.matmul(ps[:, t * D:(t + 1) * D], x1T[:, c, (2 * n + t) * T:(2 * n + t + 1) * T],
                                       wqkv[:, c, 2 * D:3 * D], start=(c == 0), stop=(c == KC - 1))
                mm.then_inc(ready, 1)

        def scores(step, u):
            t, q = u // 4, u % 4
            ps = ps_scores[u % 2]
            if u >= 2:
                pe.wait_ge(scores_taken, UNITS * step.i + u - 1)
            m, rows = q // 2, slice(64 * (q % 2), 64 * (q % 2) + 64)
            pe.matmul(ps[:, :], qT[rows, m, t * T:(t + 1) * T], kT[rows, m, :, t * T:(t + 1) * T],
                      start=True, stop=True).then_inc(scores_ready, 1)

        def turn_probs(step, u):
            i = step.i
            pe.wait_ge(probs_ready, UNITS * i + u + 1)
            for c in range(4):
                mm = pe.transpose(ps_probsT[u % 2][:, c * T:(c + 1) * T], probs[:, u % 2, c * T:(c + 1) * T], ident[:, :])
            mm.then_inc(probsT_ready, 1)

        def values(step, u):
            i, t, q = step.i, u // 4, u % 4
            pe.wait_ge(probsT_taken, UNITS * i + u + 1)
            if q == 0:
                at_least(pe, ctx_taken, G * i + t)
            for c in range(4):
                h = 4 * q + c
                mm = pe.matmul(ps_ctx[:, h * HV:(h + 1) * HV], probsT[:, u % 2, c * T:(c + 1) * T], v1[:, t, h, :],
                               start=True, stop=True)
            mm.then_inc(pv_done, 1)

        def turn_ctx(step, t):
            ps, ready = open_bank(step, "CT", t)
            pe.wait_ge(ctx_taken, G * step.i + t + 1)
            for c in range(KC):
                mm = pe.transpose(ps[:, c * T:(c + 1) * T], ctx_sb[:, t % 2, c * P:(c + 1) * P], ident[:, :])
            mm.then_inc(ready, 1)

        def project(step, t):
            ps, ready = open_bank(step, "PJ", t)
            taken(step, "CT", t)
            for c in range(KC):
                mm = pe.matmul(ps[:, 0:D], ctxT[:, t % 2, c, :], wproj[:, c, :], start=(c == 0), stop=(c == KC - 1))
            mm.then_inc(ready, 1)

        def ffn_piece(step, u):
            i = step.i
            if u < FC:
                ps, ready = open_bank(step, "F1", u)
                if u == 0:
                    pe.wait_ge(ffn_w_in, 16 * N_FFN_W * (layer_of(i - 1) + 1))
                    taken(step, "T2", 1)
                for c in range(KC):
                    mm = pe.matmul(ps[:, :], w1[:, c, u * P:(u + 1) * P], x2T[:, c, :], start=(c == 0), stop=(c == KC - 1))
                mm.then_inc(ready, 1)
                return
            t, half = (u - FC) // 2, u % 2
            if half == 0:
                open_bank(step, "F2", t)
                if t == 0:
                    taken(step, "F1", FC - 1)
            n, _ = bank_of(step, "F2", t)
            for f in range(4 * half, 4 * half + 4):
                mm = pe.matmul(ps_mm[n][:, 0:D], hidT[:, f, t * T:(t + 1) * T], w2[:, f, :],
                               start=(f == 0), stop=(f == FC - 1))
            if half == 1:
                mm.then_inc(mm_ready[n], 1)

        def run(step):
            i, attn, ffn = step.i, step.kind != "last", step.kind != "first"
            if attn:
                turn(step, "T1", xhat1, (ln1_done, i + 1))
                qkv(step)
            if ffn:
                turn(step, "T2", xhat2, (ln2_done, i))
            if attn:
                taken(step, "Q", 1)
                taken(step, "K", 1)
                scores(step, 0)
                scores(step, 1)
                taken(step, "V", 1)
            for u in range(UNITS):
                if ffn and u < UNITS - 2:
                    ffn_piece(step, u)
                if attn:
                    if u == 0:
                        scores(step, 2)
                    turn_probs(step, u)
                    if u + 3 < UNITS:
                        scores(step, u + 3)
                    if u >= 1:
                        values(step, u - 1)
                    if u >= 6 and u % 4 == 2:
                        turn_ctx(step, (u - 6) // 4)
                    if u >= 7 and u % 4 == 3:
                        project(step, (u - 7) // 4)
            if attn:
                values(step, UNITS - 1)
            if ffn:
                ffn_piece(step, UNITS - 2)
            if attn:
                turn_ctx(step, G - 1)
            if ffn:
                ffn_piece(step, UNITS - 1)
            if attn:
                project(step, G - 1)

        pe.wait_ge(consts_in, 16 * N_CONST)
        pe.wait_ge(ones_set, 1)
        run(Step("first", 0))
        with pe.Fori(1, STEPS) as i:
            run(Step("body", i))
        run(Step("last", STEPS))

    @block.scalar
    def _(act):
        def take(step, name, idx):
            n, before = bank_of(step, name, idx)
            act.wait_ge(mm_ready[n], before + 1)
            return ps_mm[n], mm_taken[n]

        def scale_turned(step, name, ln, dst):
            for c in range(KC):
                ps, taken = take(step, name, c)
                act.activation(dst[:, c, :], ps[:, :], ACT.Identity, bias=ln[:, KC + c:KC + c + 1],
                               scale=ln[:, c:c + 1]).then_inc(taken, 1)

        def keys(step):
            for m in range(KC):
                ps, taken = take(step, "K", m)
                for n in range(4):
                    last = act.activation(kT[:, m, n, :], ps[:, :], ACT.Copy, scale=head_masks[:, n:n + 1])
                last.then_inc(taken, 1)

        def exps(step, u):
            i = step.i
            act.wait_ge(shifted_ready, UNITS * i + u + 1)
            act.activation(probs[:, u % 2, :], shifted[:, u % 3, :], ACT.Exp, scale=float(D) ** -0.5).then_inc(probs_ready, 1)

        def take_probsT(step, u):
            i = step.i
            act.wait_ge(probsT_ready, UNITS * i + u + 1)
            act.activation(probsT[:, u % 2, :], ps_probsT[u % 2][:, :], ACT.Copy).then_inc(probsT_taken, 1)

        def take_ctx(step, t):
            ps, taken = take(step, "CT", t)
            act.activation(ctxT[:, t % 2, :, :].rearrange("p c t -> p (c t)"), ps[:, 0:D], ACT.Copy).then_inc(taken, 1)

        def hidden(step, c):
            ps, taken = take(step, "F1", c)
            act.activation(hidT[:, c, :], ps[:, :], ACT.Relu, bias=b1[:, c:c + 1]).then_inc(taken, 1)

        def run(step):
            i, attn, ffn = step.i, step.kind != "last", step.kind != "first"
            if attn:
                act.wait_ge(attn_w_in, 16 * N_ATTN_W * (layer_of(i) + 1))
                scale_turned(step, "T1", ln1, x1T)
                keys(step)
            if ffn:
                act.wait_ge(ffn_w_in, 16 * N_FFN_W * (layer_of(i - 1) + 1))
                scale_turned(step, "T2", ln2, x2T)
            if attn:
                exps(step, 0)
            for u in range(UNITS):
                if ffn and u < FC:
                    hidden(step, u)
                if attn:
                    if u + 1 < UNITS:
                        exps(step, u + 1)
                    take_probsT(step, u)
                    if u >= 6 and u % 4 == 2:
                        take_ctx(step, (u - 6) // 4)
            if attn:
                take_ctx(step, G - 1)

        act.wait_ge(consts_in, 16 * N_CONST)
        run(Step("first", 0))
        with act.Fori(1, STEPS) as i:
            run(Step("body", i))
        run(Step("last", STEPS))

    LINKS_STEP = 2 * 16 + UNITS + G

    @block.vector
    def _(dve):
        links, before_step = [0], [0]

        def link(ins):
            links[0] += 1
            ins.then_inc(dve_chain, 1)
            dve.wait_ge(dve_chain, before_step[0] + links[0])

        def take(step, name, idx):
            n, before = bank_of(step, name, idx)
            dve.wait_ge(mm_ready[n], before + 1)
            return ps_mm[n], mm_taken[n]

        def norm(i, dst, done):
            norm_group(dve, link, x_sb, group(i), dst, done, (stats, means, rstd, scratch, varc))

        small = (stats, means, rstd, scratch, varc)

        def norm1(i, rows, part):
            if part == 0:
                dve.wait_ge(embedded, rows)
                norm_stats(dve, link, x_sb, group(i), small)
            elif part == 1:
                norm_scale(dve, link, small)
            else:
                norm_apply(dve, x_sb, group(i), xhat1, ln1_done, small)

        def norm2(step):
            n, per = (len(step_uses("body")) - 1) % NBANK, len(step_uses("body")) // NBANK
            firsts = sum(1 for at, use in enumerate(step_uses("first")) if use and at % NBANK == n)
            dve.wait_ge(mm_taken[n], firsts + (step.i - 1) * per)
            norm(step.i - 1, xhat2, ln2_done)

        def softmax_shift(step, u):
            i = step.i
            ps = ps_scores[u % 2][:, :].rearrange("p (h s) -> p h s", h=4)
            mx = rowmax[:, u % 3, :]
            dve.wait_ge(scores_ready, UNITS * i + u + 1)
            masked = shifted[:, u % 3, :].rearrange("p (h s) -> p h s", h=4)
            dve.tensor_tensor(masked, ps, causal[:, :].unsqueeze(1).to_broadcast([P, 4, T]), ALU.add).then_inc(scores_taken, 1)
            dve.wait_ge(scores_taken, UNITS * i + u + 1)
            link(dve.tensor_reduce(mx, masked, AX.X, ALU.max))
            dve.tensor_tensor(masked, masked, mx.unsqueeze(2).to_broadcast([P, 4, T]),
                              ALU.subtract).then_inc(shifted_ready, 1)

        def take_context(step, t):
            i = step.i
            dve.wait_ge(pv_done, UNITS * i + 4 * t + 4)
            ps = ps_ctx[:, 0:HEADS * HV].rearrange("p (h v) -> p h v", v=HV)
            link(dve.reciprocal(rsum[:, :], ps[:, :, HD]))
            dve.tensor_tensor(ctx_sb[:, t % 2, :].rearrange("p (h v) -> p h v", v=HD), ps[:, :, 0:HD],
                              rsum[:, :].unsqueeze(2).to_broadcast([P, HEADS, HD]), ALU.mult).then_inc(ctx_taken, 1)

        def add_projection(step, t):
            xt = x_sb[:, group(step.i) * G + t, :]
            ps, taken = take(step, "PJ", t)
            if t == 0:
                dve.wait_ge(bproj_added, step.i + 1)
            dve.tensor_tensor(xt, ps[:, 0:D], xt, ALU.add).then_inc(taken, 1)

        def add_ffn(step, t):
            xt = x_sb[:, group(step.i - 1) * G + t, :]
            ps, taken = take(step, "F2", t)
            if t == 0:
                dve.wait_ge(b2_added, step.i)
            dve.tensor_tensor(xt, ps[:, 0:D], xt, ALU.add).then_inc(taken, 1)

        def run(step):
            i, attn, ffn = step.i, step.kind != "last", step.kind != "first"
            if attn:
                for m in range(KC):
                    ps, taken = take(step, "Q", m)
                    dve.tensor_copy(qT[:, m, :], ps[:, :]).then_inc(taken, 1)
            if ffn:
                norm2(step)
            if attn:
                for n in range(2):
                    ps, taken = take(step, "V", n)
                    dve.tensor_copy(v1[:, 2 * n:2 * n + 2, :, 0:HD].rearrange("p t h v -> p (t h) v"),
                                    ps[:, :].rearrange("p (h v) -> p h v", v=HD)).then_inc(taken, 1)
                softmax_shift(step, 0)
                softmax_shift(step, 1)
            for u in range(UNITS):
                if attn:
                    if u + 2 < UNITS:
                        softmax_shift(step, u + 2)
                    if u >= 5 and u % 4 == 1:
                        take_context(step, (u - 5) // 4)
                    if u >= 8 and u % 4 == 0:
                        add_projection(step, (u - 8) // 4)
                    if 9 <= u < 12:
                        norm1(i + 1, 2 * G if step.kind == "first" else B, u - 9)
                if ffn and u >= FC and u % 2 == 1 and u < UNITS - 1:
                    add_ffn(step, (u - FC) // 2)
            if attn:
                add_projection(step, G - 2)
                take_context(step, G - 1)
            if ffn:
                add_ffn(step, G - 1)
            if attn:
                add_projection(step, G - 1)

        dve.wait_ge(consts_in, 16 * N_CONST)
        for part in range(3):
            norm1(0, G, part)
        run(Step("first", 0))
        head, links[0] = links[0], 0
        with dve.Fori(1, STEPS) as i:
            before_step[0] = head + (i - 1) * LINKS_STEP
            run(Step("body", i))
        assert links[0] == LINKS_STEP
        before_step[0], links[0] = head + (STEPS - 1) * LINKS_STEP, 0
        run(Step("last", STEPS))


class Banks:

    def __init__(self, nc, ctx, tag, uses, n=8):
        self.ps = [ctx.enter_context(nc.psum_tensor(f"ps_{tag}{k}", [P, 512], F32)) for k in range(n)]
        self.ready = [ctx.enter_context(nc.semaphore(f"{tag}_ready{k}")) for k in range(n)]
        self.taken = [ctx.enter_context(nc.semaphore(f"{tag}_taken{k}")) for k in range(n)]
        self.at = {use: k for k, use in enumerate(uses)}
        self.uses, self.n = uses, n
        self.per = [len(range(k, len(uses), n)) for k in range(n)]

    def count(self, use, r):
        k = self.at[use]
        return k % self.n, r * self.per[k % self.n] + k // self.n


class BodyBanks:

    def __init__(self, nc, ctx, tag, uses, prep, n=8):
        self.ps = [ctx.enter_context(nc.psum_tensor(f"ps_{tag}{k}", [P, 512], F32)) for k in range(n)]
        self.ready = [ctx.enter_context(nc.semaphore(f"{tag}_ready{k}")) for k in range(n)]
        self.taken = [ctx.enter_context(nc.semaphore(f"{tag}_taken{k}")) for k in range(n)]
        self.at = {use: k for k, use in enumerate(uses)}
        self.uses, self.prep, self.n = uses, prep, n

    def count(self, use, step):
        at = self.at[use]
        k = at % self.n
        there = [at2 for at2 in range(k, len(self.uses), self.n)
                 if step.kind == "body" or (self.uses[at2][0] in self.prep) == (step.kind == "first")]
        before = sum(1 for at2 in there if at2 < at)
        if step.kind == "first":
            return k, before
        firsts = sum(1 for at2 in range(k, len(self.uses), self.n) if self.uses[at2][0] in self.prep)
        per = len(range(k, len(self.uses), self.n))
        return k, firsts + (step.i - 1) * per + before


LA_HEADS, LA_D = 8, 32
LEVELS = [1, 2, 4, 8, 16, 32, 64]
MASK_LEVELS = 4
COMPS = ["are", "aim", "kre", "kim", "qre", "qim"]
TILES = LA_HEADS // 2
LA_ROUNDS = B // G


def linear_attention(nc, ctx, x_sb, ins, consts):
    def sb(name, shape, dt=F32):
        return ctx.enter_context(nc.sbuf_tensor(name, shape, dt))

    def sem(name):
        return ctx.enter_context(nc.semaphore(name))

    ident = consts[0]
    N2 = KC * GT

    w_in = sb("w_in", [P, KC, D])
    w_comp = sb("w_comp", [P, KC, len(COMPS) * D])
    w_v = sb("w_v", [P, KC, 2 * D])
    w_y = sb("w_y", [P, 2 * KC, D])
    w_out = sb("w_out", [P, KC, D])
    h0 = sb("h0", [P, TILES, 2 * LA_D])
    bias_cols = sb("bias_cols", [P, 2 * len(COMPS) + 2 * KC])
    v_bias = sb("v_bias", [P, 2 * D])
    out_bias = sb("out_bias", [P, D])
    level_masks = sb("level_masks", [P, MASK_LEVELS, T // 2], U32)

    stats = sb("la_stats", [P, G, 6])
    means = sb("la_means", [P, G, 1])
    rstd = sb("la_rstd", [P, G, 1])
    scratch = sb("la_scratch", [P, G, 1])
    varc = sb("la_varc", [P, G, 1])

    spare = sb("spare", [P, 4 * N2])
    tmp = [spare[:, n * N2:(n + 1) * N2] for n in range(4)]
    xhat = tmp[0].rearrange("p (g d) -> p g d", g=G)
    xT = tmp[1].rearrange("p (c t) -> p c t", c=KC)
    raw = {comp: sb("raw_" + comp, [P, N2]) for comp in COMPS}
    raw = {comp: whole[:, :] for comp, whole in raw.items()}
    neg_qim = tmp[3]
    key_tmp = [sb(f"key_tmp{n}", [P, GT]) for n in range(4)]
    s_all = sb("s_all", [P, LA_HEADS, G, 2, T])
    y_sb = [s_all[:, 0:KC, g] for g in range(G)]
    uT = sb("uT", [P, KC, GT])
    zT = sb("zT", [P, KC, GT])
    decay = sb("decay", [P, N2])
    q12 = sb("q12", [P, 2, TILES, GT])
    k12 = sb("k12", [P, TILES, GT])
    totals = sb("totals", [P, 2 * TILES * GT])
    values = sb("values", [P, G * LA_HEADS * 3 * LA_D])
    v_sb = values[:, :].rearrange("p (g h e) -> p g h e", g=G, h=LA_HEADS)
    yT = values[:, 0:2 * N2].rearrange("p (c t) -> p c t", c=2 * KC)

    def total(m):
        n = TILES * GT
        at = 2 * n - 2 * n // m
        return totals[:, at:at + n // m]

    parts = [(comp, m) for comp in COMPS for m in range(KC)]
    scored = [("D", h, pair) for h in range(LA_HEADS) for pair in range(2)]
    scored += [("S", m, h) for m in LEVELS for h in range(LA_HEADS)]
    FIRST_PARTS = 2 * KC
    uses = [("T", c) for c in range(KC)] + [("U", m) for m in range(KC)] + parts[:FIRST_PARTS]
    for n, use in enumerate(scored):
        uses.append(use)
        if n % 5 == 4 and n // 5 < len(parts) - FIRST_PARTS:
            uses.append(parts[FIRST_PARTS + n // 5])
    uses += [("Y", g) for g in range(G)] + [("YT", g) for g in range(G)]
    uses += [("V", 0)] + [("Z", m) for m in range(KC)] + [("V", g) for g in range(1, G)] + [("O", g) for g in range(G)]
    banks = BodyBanks(nc, ctx, "la", uses, ("T", "U", "V") + tuple(COMPS))

    weights_in = sem("la_weights_in")
    ln_done = sem("la_ln_done")
    bias_added = sem("la_bias_added")
    squares_ready = sem("squares_ready")
    mag_ready = sem("mag_ready")
    root_ready = sem("root_ready")
    phases_ready = sem("phases_ready")
    products_ready = sem("products_ready")
    decay_ready = sem("decay_ready")
    q_ready = sem("q_ready")
    k_ready = sem("k_ready")
    negq_ready = sem("negq_ready")
    decay_stacked = sem("decay_stacked")
    q_stacked = sem("q_stacked")
    k_stacked = sem("k_stacked")
    totals_ready = sem("totals_ready")
    q_scaled = sem("q_scaled")
    q_scaled_late = sem("q_scaled_late")
    key_chain = sem("key_chain")
    k_scaled = sem("k_scaled")
    v_ready = sem("v_ready")
    starts_used = sem("starts_used")
    norm_chain = sem("la_norm_chain")
    chain = sem("la_chain")
    passed = sem("la_passed")

    N_W = 10
    N_TOTALS = len(LEVELS) - 1
    LATE = MASK_LEVELS + 1
    N_Q_SCALED, N_Q_LATE = TILES * LATE, TILES * (len(LEVELS) + 1 - LATE)
    N_K_SCALED = TILES * (len(LEVELS) - 1)
    block = ctx.enter_context(nc.Block())

    def blocks(ap, m):
        return ap.rearrange("p (n s m) -> p n s m", s=2, m=m)

    @block.sync
    def _(sp):
        sp.dma_start(w_in[:, :, :], ins["la_w_in"].rearrange("(c p) n -> p c n", p=P)).then_inc(weights_in, 16)
        sp.dma_start(w_comp[:, :, :], ins["la_w_comp"].rearrange("(c p) n -> p c n", p=P)).then_inc(weights_in, 16)
        sp.dma_start(w_v[:, :, :], ins["la_w_v"].rearrange("(c p) n -> p c n", p=P)).then_inc(weights_in, 16)
        sp.dma_start(w_y[:, :, :], ins["la_w_y"].rearrange("(c p) n -> p c n", p=P)).then_inc(weights_in, 16)
        sp.dma_start(w_out[:, :, :], ins["la_w_out"].rearrange("(c p) n -> p c n", p=P)).then_inc(weights_in, 16)
        sp.dma_start(h0[:, :, :], ins["la_h0"]).then_inc(weights_in, 16)
        sp.dma_start(bias_cols[:, :], ins["la_bias_cols"]).then_inc(weights_in, 16)
        sp.dma_start(v_bias[:, :], ins["la_v_bias"].to_broadcast([P, 2 * D])).then_inc(weights_in, 16)
        sp.dma_start(out_bias[:, :], ins["la_out_bias"].to_broadcast([P, D])).then_inc(weights_in, 16)
        sp.dma_start(level_masks[:, :, :], ins["la_masks"]).then_inc(weights_in, 16)

        def stack(dst, src, imaginary, done):
            src = src.rearrange("p (c t) -> p c t", c=KC)
            for j in range(4):
                rows = 64 * (j % 2) + 32 * imaginary
                sp.dma_start(dst[rows:rows + 32, j // 2:TILES:2, :], src[32 * j:32 * j + 32, :, :]).then_inc(done, 16)

        def body(step):
            i = step.i
            this, keys_count, stood = i + 1, KC * (i + 1), i
            if step.kind == "body":
                q_count, k_count = N_Q_SCALED * (i - 1) + 2 * TILES, N_K_SCALED * (i - 1) + TILES
                k, before = banks.count(("S", LEVELS[-1], LA_HEADS - 1), step)
                last_scores = before + 1
            sp.wait_ge(decay_ready, this)
            if step.kind == "body":
                sp.wait_ge(q_scaled, q_count)
                sp.wait_ge(k_scaled, k_count)
            for part in range(2):
                stack(total(1).rearrange("p (c t) -> p c t", c=TILES), decay[:, :], part, decay_stacked)
            sp.wait_ge(q_ready, this)
            if step.kind == "body":
                sp.wait_ge(starts_used, stood)
            stack(q12[:, 0], raw["qre"], 0, q_stacked)
            stack(q12[:, 1], raw["qre"], 1, q_stacked)
            stack(q12[:, 1], raw["qim"], 0, q_stacked)
            sp.wait_ge(negq_ready, this)
            stack(q12[:, 0], neg_qim, 1, q_stacked)
            sp.wait_ge(k_ready, keys_count)
            if step.kind == "body":
                sp.wait_ge(banks.ready[k], last_scores)
            stack(k12, raw["kre"], 0, k_stacked)
            stack(k12, raw["kim"], 1, k_stacked)

        body(Step("first", 0))
        with sp.Fori(1, LA_ROUNDS) as i:
            body(Step("body", i))

    @block.tensor
    def _(pe):
        pe.wait_ge(weights_in, 16 * N_W)

        def body(step):
            i = step.i

            def open_bank(use):
                n, before = banks.count(use, step)
                pe.wait_ge(banks.taken[n], before + 1)
                return banks.ps[n], banks.ready[n]

            def taken(use):
                n, before = banks.count(use, step)
                pe.wait_ge(banks.taken[n], before + 2)

            def turn(c):
                ps, ready = open_bank(("T", c))
                if c == 0:
                    pe.wait_ge(ln_done, i + 1)
                for g in range(G):
                    mm = pe.transpose(ps[:, g * T:(g + 1) * T], xhat[:, g, c * P:(c + 1) * P], ident[:, :])
                mm.then_inc(ready, 1)

            def product_in(m):
                ps, ready = open_bank(("U", m))
                if m == 0:
                    taken(("T", 1))
                for c in range(KC):
                    mm = pe.matmul(ps[:, :], w_in[:, c, m * P:(m + 1) * P], xT[:, c, :], start=(c == 0), stop=(c == KC - 1))
                mm.then_inc(ready, 1)

            def component(comp, m):
                n = COMPS.index(comp)
                ps, ready = open_bank((comp, m))
                if n == 0 and m == 0:
                    taken(("U", KC - 1))
                for c in range(KC):
                    mm = pe.matmul(ps[:, :], w_comp[:, c, n * D + m * P:n * D + (m + 1) * P], uT[:, c, :],
                                   start=(c == 0), stop=(c == KC - 1))
                mm.then_inc(ready, 1)

            def value(g):
                ps, ready = open_bank(("V", g))
                for c in range(KC):
                    mm = pe.matmul(ps[:, :], uT[:, c, g * T:(g + 1) * T], w_v[:, c, :], start=(c == 0), stop=(c == KC - 1))
                mm.then_inc(ready, 1)

            def own_scores(h, pair):
                rows, c = slice(64 * (h % 2), 64 * (h % 2) + 64), h // 2
                ps, ready = open_bank(("D", h, pair))
                if h == 0 and pair == 0:
                    pe.wait_ge(k_stacked, 16 * 8 * i)
                    pe.wait_ge(q_stacked, 16 * 16 * i)
                for n in range(2):
                    tok = slice((2 * pair + n) * T, (2 * pair + n + 1) * T)
                    mm = pe.matmul(ps[:, n * 2 * T:(n + 1) * 2 * T], k12[rows, c, tok], q12[rows, :, c, tok],
                                   start=True, stop=True)
                mm.then_inc(ready, 1)

            def level_scores(m, h):
                n = LEVELS.index(m)
                rows, c = slice(64 * (h % 2), 64 * (h % 2) + 64), h // 2
                ps, ready = open_bank(("S", m, h))
                if h % 2 == 0:
                    if n < LATE:
                        pe.wait_ge(q_scaled, N_Q_SCALED * (i - 1) + TILES * n + c + 1)
                    else:
                        pe.wait_ge(q_scaled_late, N_Q_LATE * (i - 1) + TILES * (n - LATE) + c + 1)
                    if n > 0:
                        pe.wait_ge(k_scaled, N_K_SCALED * (i - 1) + TILES * (n - 1) + c + 1)
                for g in range(G):
                    tok = slice(g * T, (g + 1) * T)
                    right = q12[rows, :, c, tok].rearrange("p i (n s m) -> p i n s m", s=2, m=m)[:, :, :, 1, :]
                    mm = pe.matmul(ps[:, g * T:(g + 1) * T], k12[rows, c, tok], right, start=True, stop=True)
                mm.then_inc(ready, 1)

            def outputs():
                opened = []
                for g in range(G):
                    opened.append(open_bank(("Y", g)))
                    if g == 0:
                        pe.wait_ge(q_scaled_late, N_Q_LATE * i)
                    tok = slice(g * T, (g + 1) * T)
                    for n in range(2):
                        for c in range(TILES):
                            mm = pe.matmul(opened[g][0][:, n * D + c * 64:n * D + (c + 1) * 64], q12[:, n, c, tok],
                                           h0[:, c, :], start=(n == 0 and c == 0), stop=False, skip_group_check=True)
                mm.then_inc(starts_used, 1)
                taken(("S", LEVELS[MASK_LEVELS - 1], LA_HEADS - 1))
                taken(("S", LEVELS[-1], LA_HEADS - 1))
                pe.wait_ge(v_ready, G * i)
                for g in range(G):
                    ps, ready = opened[g]
                    out = ps[:, :].rearrange("p (i h e) -> p i h e", i=2, h=LA_HEADS)
                    for h in range(LA_HEADS):
                        for n in range(2):
                            at = LA_D * (1 - n)
                            mm = pe.matmul(out[:, :, h, :], s_all[:, h, g, n, :], v_sb[:, g, h, at:at + 2 * LA_D],
                                           start=False, stop=(h == LA_HEADS - 1 and n == 1), skip_group_check=True)
                    mm.then_inc(ready, 1)
                    if g > 0:
                        turn_output(g - 1)
                turn_output(G - 1)

            def turn_output(g):
                ps, ready = open_bank(("YT", g))
                taken(("Y", g))
                for c in range(2 * KC):
                    mm = pe.transpose(ps[:, c * T:(c + 1) * T], y_sb[g][:, c // 2, c % 2, :], ident[:, :])
                mm.then_inc(ready, 1)

            def gate_product(m):
                ps, ready = open_bank(("Z", m))
                if m == 0:
                    taken(("YT", G - 1))
                for c in range(2 * KC):
                    mm = pe.matmul(ps[:, :], w_y[:, c, m * P:(m + 1) * P], yT[:, c, :], start=(c == 0), stop=(c == 2 * KC - 1))
                mm.then_inc(ready, 1)

            def product_out(g):
                ps, ready = open_bank(("O", g))
                if g == 0:
                    taken(("Z", KC - 1))
                for c in range(KC):
                    mm = pe.matmul(ps[:, 0:D], zT[:, c, g * T:(g + 1) * T], w_out[:, c, :], start=(c == 0), stop=(c == KC - 1))
                mm.then_inc(ready, 1)

            for use in uses:
                name = use[0]
                if step.kind != "body" and (name in banks.prep) != (step.kind == "first"):
                    continue
                if name == "T":
                    turn(use[1])
                elif name == "U":
                    product_in(use[1])
                elif name == "V":
                    value(use[1])
                elif name == "D":
                    own_scores(use[1], use[2])
                elif name == "S":
                    level_scores(use[1], use[2])
                elif use == ("Y", 0):
                    outputs()
                elif name == "Z":
                    gate_product(use[1])
                elif name == "O":
                    product_out(use[1])
                elif name in COMPS:
                    component(name, use[1])

        body(Step("first", 0))
        with pe.Fori(1, LA_ROUNDS) as i:
            body(Step("body", i))
        body(Step("last", LA_ROUNDS))

    @block.scalar
    def _(act):
        act.wait_ge(weights_in, 16 * N_W)

        def body(step):
            i = step.i

            def take(use):
                n, before = banks.count(use, step)
                act.wait_ge(banks.ready[n], before + 1)
                return banks.ps[n], banks.taken[n]

            def gated(name, dst, first):
                for m in range(KC):
                    ps, taken = take((name, m))
                    col = 2 * len(COMPS) + first + m
                    act.activation(dst[:, m, :], ps[:, :], ACT.Silu, bias=bias_cols[:, col:col + 1]).then_inc(taken, 1)

            def components(*comps):
                for comp in comps:
                    n = COMPS.index(comp)
                    for m in range(KC):
                        ps, taken = take((comp, m))
                        act.activation(raw[comp][:, m * GT:(m + 1) * GT], ps[:, :], ACT.Identity,
                                       bias=bias_cols[:, KC * n + m:KC * n + m + 1]).then_inc(taken, 1)

            if step.kind != "last":
                for c in range(KC):
                    ps, taken = take(("T", c))
                    act.activation(xT[:, c, :], ps[:, :], ACT.Copy).then_inc(taken, 1)
                gated("U", uT, 0)
                if step.kind == "body":
                    act.wait_ge(k_stacked, 16 * 8 * i)
                    act.wait_ge(q_stacked, 16 * 16 * i)
                components("are", "aim")
                n, before = banks.count(("aim", 1), step)
                act.wait_ge(banks.taken[n], before + 2)
                act.activation(tmp[0], raw["are"], ACT.Square)
                act.activation(tmp[1], raw["aim"], ACT.Square).then_inc(squares_ready, 1)
                components("kre", "kim", "qre", "qim")
                act.wait_ge(mag_ready, i + 1)
                act.activation(tmp[3], tmp[2], ACT.Sqrt).then_inc(root_ready, 1)
            if step.kind == "first":
                return
            for m in LEVELS[MASK_LEVELS:]:
                for h in range(LA_HEADS):
                    ps, taken = take(("S", m, h))
                    src = ps[:, :].rearrange("p (g i t) -> p g i t", g=G, i=2)
                    for b in range(T // (2 * m)):
                        rows = slice(2 * m * b, 2 * m * b + m)
                        last = act.activation(s_all[rows, h, :, :, 2 * m * b + m:2 * m * (b + 1)],
                                              src[rows, :, :, m * b:m * (b + 1)], ACT.Copy)
                    last.then_inc(taken, 1)
            for g in range(G):
                ps, taken = take(("Y", g))
                act.activation(y_sb[g], ps[:, :].rearrange("p (h i t) -> p h i t", h=KC, i=2), ACT.Copy).then_inc(taken, 1)
            for g in range(G):
                ps, taken = take(("YT", g))
                act.activation(yT[:, :, g * T:(g + 1) * T], ps[:, :].rearrange("p (c t) -> p c t", c=2 * KC),
                               ACT.Copy).then_inc(taken, 1)
            gated("Z", zT, KC)

        body(Step("first", 0))
        with act.Fori(1, LA_ROUNDS) as i:
            body(Step("body", i))
        body(Step("last", LA_ROUNDS))

    @block.gpsimd
    def _(pool):
        pool.wait_ge(weights_in, 16 * N_W)

        def add_bias(r):
            xg = x_sb[:, bass.ds(r * G, G), :]
            pool.wait_ge(ln_done, r + 1)
            pool.tensor_tensor(xg, xg, out_bias[:, :].unsqueeze(1).to_broadcast([P, G, D]), ALU.add).then_inc(bias_added, 1)

        def block_totals(step):
            i = step.i
            if step.kind == "body":
                pool.wait_ge(q_scaled, N_Q_SCALED * i)
                pool.wait_ge(q_scaled_late, N_Q_LATE * i)
            pool.wait_ge(decay_stacked, 16 * 8 * (i + 1))
            for n, m in enumerate(LEVELS[:-1]):
                pairs = total(m).rearrange("p (n s) -> p n s", s=2)
                if n > 0:
                    pool.wait_ge(totals_ready, N_TOTALS * i + n)
                pool.tensor_tensor(total(2 * m), pairs[:, :, 0], pairs[:, :, 1], ALU.mult).then_inc(totals_ready, 1)

        def scale(step):
            pool.wait_ge(totals_ready, N_TOTALS * step.i)
            for n, m in enumerate(LEVELS):
                for c in range(TILES):
                    k, before = banks.count(("S", m, 2 * c + 1), step)
                    pool.wait_ge(banks.ready[k], before + 1)
                    nb = GT // (2 * m)
                    if n + 1 >= LATE:
                        for half in range(2):
                            q = blocks(q12[:, half, c, :], m)[:, :, 1, :]
                            left_total = total(m).rearrange("p (c n s) -> p c n s", c=TILES, s=2)[:, c, :, 0]
                            last = pool.tensor_tensor(q, q, left_total.unsqueeze(2).to_broadcast([P, nb, m]), ALU.mult)
                        last.then_inc(q_scaled_late, 1)
                    if n + 1 < len(LEVELS):
                        left = blocks(k12[:, c, :], m)[:, :, 0, :]
                        right_total = total(m).rearrange("p (c n s) -> p c n s", c=TILES, s=2)[:, c, :, 1]
                        pool.tensor_tensor(left, left, right_total.unsqueeze(2).to_broadcast([P, nb, m]),
                                           ALU.mult).then_inc(k_scaled, 1)

        def turn_keys(step):
            i = step.i
            k, before = banks.count(("kim", 1), step)
            pool.wait_ge(banks.taken[k], before + 2)
            pool.wait_ge(products_ready, i + 1)
            for c in range(KC):
                chunk = slice(c * GT, (c + 1) * GT)
                re, im, p_re, p_im = (raw[name][:, chunk] for name in ("kre", "kim", "are", "aim"))
                pool.tensor_tensor(key_tmp[0][:, :], re, p_re, ALU.mult)
                pool.tensor_tensor(key_tmp[1][:, :], im, p_im, ALU.mult)
                pool.tensor_tensor(key_tmp[2][:, :], im, p_re, ALU.mult)
                pool.tensor_tensor(key_tmp[3][:, :], re, p_im, ALU.mult).then_inc(key_chain, 1)
                pool.wait_ge(key_chain, KC * i + c + 1)
                pool.tensor_tensor(re, key_tmp[0][:, :], key_tmp[1][:, :], ALU.add)
                pool.tensor_tensor(im, key_tmp[2][:, :], key_tmp[3][:, :], ALU.subtract).then_inc(k_ready, 1)
                pool.wait_ge(k_ready, KC * i + c + 1)

        add_bias(0)
        turn_keys(Step("first", 0))
        block_totals(Step("first", 0))
        with pool.Fori(1, LA_ROUNDS) as i:
            add_bias(i)
            scale(Step("body", i))
            turn_keys(Step("body", i))
            block_totals(Step("body", i))
        scale(Step("last", LA_ROUNDS))

    @block.vector
    def _(dve):
        dve.wait_ge(weights_in, 16 * N_W)
        for n in range(8):
            dve.sem_inc(banks.taken[n], 1)
        NORM_LINKS, LINKS = 16, 6 + 2 * len(LEVELS)
        links = [0]

        def norm(r):
            links[0] = 0

            def link(ins):
                links[0] += 1
                ins.then_inc(norm_chain, 1)
                dve.wait_ge(norm_chain, r * NORM_LINKS + links[0])
            norm_group(dve, link, x_sb, r, xhat, ln_done, (stats, means, rstd, scratch, varc))
            assert links[0] == NORM_LINKS, links[0]

        def body(step, with_norm):
            i = step.i
            links[0] = 0

            def link(ins):
                links[0] += 1
                ins.then_inc(chain, 1)
                dve.wait_ge(chain, i * LINKS + links[0])

            def take(use):
                n, before = banks.count(use, step)
                dve.wait_ge(banks.ready[n], before + 1)
                return banks.ps[n], banks.taken[n]

            def evacuated(use):
                n, before = banks.count(use, step)
                dve.wait_ge(banks.taken[n], before + 2)

            mag2 = tmp[2]

            def magnitudes():
                dve.wait_ge(squares_ready, i + 1)
                dve.tensor_tensor(mag2, tmp[0], tmp[1], ALU.add).then_inc(mag_ready, 1)
                dve.wait_ge(mag_ready, i + 1)

            def decays():
                link(dve.tensor_scalar(tmp[0], mag2, 1.0, None, ALU.add))
                link(dve.reciprocal(tmp[0], tmp[0]))
                dve.tensor_tensor(decay[:, :], mag2, tmp[0], ALU.mult).then_inc(decay_ready, 1)
                dve.wait_ge(decay_ready, i + 1)

            def phases():
                dve.wait_ge(root_ready, i + 1)
                link(dve.reciprocal(tmp[1], tmp[3]))
                link(dve.scalar_tensor_tensor(tmp[0], tmp[1], -0.5, tmp[1], ALU.mult, ALU.mult))
                link(dve.tensor_tensor(tmp[0], tmp[0], mag2, ALU.mult))
                link(dve.scalar_tensor_tensor(tmp[1], tmp[0], 1.5, tmp[1], ALU.add, ALU.mult))

            def unit_phases():
                dve.tensor_tensor(raw["are"], raw["are"], tmp[1], ALU.mult)
                dve.tensor_tensor(raw["aim"], raw["aim"], tmp[1], ALU.mult).then_inc(phases_ready, 1)
                dve.wait_ge(phases_ready, i + 1)

            def running_product(m):
                nb = N2 // (2 * m)

                def carry(ap):
                    return blocks(ap, m)[:, :, 0, m - 1:m].to_broadcast([P, nb, m])

                def right(ap):
                    return blocks(ap, m)[:, :, 1, :]

                def part(n):
                    return tmp[n][:, 0:N2 // 2].rearrange("p (n m) -> p n m", m=m)
                dve.tensor_tensor(part(0), right(raw["are"]), carry(raw["are"]), ALU.mult)
                dve.tensor_tensor(part(1), right(raw["aim"]), carry(raw["aim"]), ALU.mult)
                dve.tensor_tensor(part(2), right(raw["are"]), carry(raw["aim"]), ALU.mult)
                link(dve.tensor_tensor(part(3), right(raw["aim"]), carry(raw["are"]), ALU.mult))
                dve.tensor_tensor(right(raw["are"]), part(0), part(1), ALU.subtract)
                last = dve.tensor_tensor(right(raw["aim"]), part(2), part(3), ALU.add)
                if m < LEVELS[-1]:
                    link(last)
                else:
                    last.then_inc(products_ready, 1)
                    dve.wait_ge(products_ready, i + 1)

            def turn_queries():
                evacuated(("qim", 1))
                re, im = raw["qre"], raw["qim"]
                dve.tensor_tensor(tmp[0], re, raw["are"], ALU.mult)
                dve.tensor_tensor(tmp[1], im, raw["aim"], ALU.mult)
                dve.tensor_tensor(tmp[2], im, raw["are"], ALU.mult)
                link(dve.tensor_tensor(tmp[3], re, raw["aim"], ALU.mult))
                dve.tensor_tensor(re, tmp[0], tmp[1], ALU.subtract)
                dve.tensor_tensor(im, tmp[2], tmp[3], ALU.add).then_inc(q_ready, 1)
                dve.wait_ge(q_ready, i + 1)
                dve.tensor_scalar(neg_qim, im, -1.0, None, ALU.mult).then_inc(negq_ready, 1)

            def take_values(g):
                ps, taken = take(("V", g))
                src = ps[:, :].rearrange("p (h e) -> p h e", h=LA_HEADS)
                bias = v_bias[:, :].rearrange("p (h e) -> p h e", h=LA_HEADS)
                dve.tensor_tensor(v_sb[:, g, :, LA_D:3 * LA_D], src, bias, ALU.add)
                dve.scalar_tensor_tensor(v_sb[:, g, :, 0:LA_D], src[:, :, LA_D:2 * LA_D], -1.0,
                                         bias[:, :, LA_D:2 * LA_D], ALU.mult, ALU.subtract).then_inc(v_ready, 1)
                dve.wait_ge(v_ready, G * i + g + 1)
                dve.sem_inc(taken, 1)

            def scale_queries(n, c):
                if n == 0:
                    if c == 0:
                        dve.wait_ge(decay_stacked, 16 * 8 * i)
                    take(("D", 2 * c + 1, 1))
                    q = q12[:, :, c, :]
                    one = total(1).rearrange("p (c t) -> p c t", c=TILES)[:, c, :]
                    dve.tensor_tensor(q, q, one.unsqueeze(1).to_broadcast([P, 2, GT]), ALU.mult).then_inc(q_scaled, 1)
                    return
                m = LEVELS[n - 1]
                nb = GT // (2 * m)
                if n == 1 and c == 0:
                    dve.wait_ge(totals_ready, N_TOTALS * i)
                take(("S", m, 2 * c + 1))
                for half in range(2):
                    q = blocks(q12[:, half, c, :], m)[:, :, 1, :]
                    left_total = total(m).rearrange("p (c n s) -> p c n s", c=TILES, s=2)[:, c, :, 0]
                    last = dve.tensor_tensor(q, q, left_total.unsqueeze(2).to_broadcast([P, nb, m]), ALU.mult)
                last.then_inc(q_scaled, 1)

            def own_tile(c):
                for h in (2 * c, 2 * c + 1):
                    for pair in range(2):
                        ps, taken = take(("D", h, pair))
                        dst = s_all[:, h, 2 * pair:2 * pair + 2, :, :].rearrange("p g i t -> p (g i) t")
                        dve.tensor_tensor(dst, ps[:, :].rearrange("p (n t) -> p n t", n=4),
                                          ident[:, :].unsqueeze(1).to_broadcast([P, 4, T]), ALU.mult).then_inc(taken, 1)
                scale_queries(0, c)

            def level_tile(n, c):
                m = LEVELS[n]
                scale_queries(n + 1, c)
                for h in (2 * c, 2 * c + 1):
                    ps, taken = take(("S", m, h))
                    dve.sem_inc(passed, 1)
                    dst = s_all[:, h].rearrange("p g i (n s m) -> p (g i) n s m", s=2, m=m)[:, :, :, 1, :]
                    mask = level_masks[:, n, :].rearrange("p (n m) -> p n m", m=m)
                    dve.copy_predicated(dst, mask.unsqueeze(1).to_broadcast([P, 2 * G, T // (2 * m), m]),
                                        ps[:, :].rearrange("p (a n m) -> p a n m", a=2 * G, m=m)).then_inc(taken, 1)

            if step.kind != "first":
                for c in range(TILES):
                    own_tile(c)
                for n in range(MASK_LEVELS):
                    for c in range(TILES):
                        level_tile(n, c)
            if step.kind != "last":
                magnitudes()
                decays()
                phases()
                unit_phases()
                for m in LEVELS:
                    running_product(m)
                turn_queries()
                if with_norm:
                    norm(i + 1)
            if step.kind != "last":
                if step.kind == "body":
                    take(("Z", KC - 1))
                for g in range(G):
                    take_values(g)
            if step.kind != "first":
                dve.wait_ge(bias_added, i)
                for g in range(G):
                    xt = x_sb[:, (i - 1) * G + g, :]
                    ps, taken = take(("O", g))
                    dve.tensor_tensor(xt, ps[:, 0:D], xt, ALU.add).then_inc(taken, 1)

        norm(0)
        body(Step("first", 0), True)
        with dve.Fori(1, LA_ROUNDS - 1) as i:
            body(Step("body", i), True)
        body(Step("body", LA_ROUNDS - 1), False)
        body(Step("last", LA_ROUNDS), False)


EXPERTS, CAP = 8, B * T // 8
SLOTS = EXPERTS * CAP
CG = CAP // P


def experts(nc, ctx, x_sb, ins, consts, out):
    def sb(name, shape, dt=F32):
        return ctx.enter_context(nc.sbuf_tensor(name, shape, dt))

    def sem(name):
        return ctx.enter_context(nc.semaphore(name))

    ident = consts[0]
    slots_in = nc.dram_tensor("slots_in", [2 * SLOTS, D], F32, kind="Internal").ap()
    slots_out = nc.dram_tensor("slots_out", [SLOTS, D], F32, kind="Internal").ap()

    w1 = sb("ex_w1", [P, 2, KC, FF])
    w2 = sb("ex_w2", [P, 2, FC, D])
    w_r = sb("w_r", [P, KC, EXPERTS])
    before = sb("before", [P, P])
    ones = sb("ones", [P, P])
    countdown = sb("countdown", [P, EXPERTS])
    spill_row = sb("spill_row", [P, B])
    zeros = sb("zeros", [P, SLOTS * D // P // 8])
    xn = sb("xn", [P, B, D])
    xnT = sb("xnT", [P, KC, GT])
    xn_group = sb("xn_group", [P, G, D])
    small = [sb("ex_stats", [P, G, 6])] + [sb(f"ex_small{n}", [P, G, 1]) for n in range(4)]
    logits = sb("logits", [P, B, EXPERTS])
    top = sb("top", [P, B])
    expd = sb("ex_expd", [P, B, EXPERTS])
    hit = sb("hit", [P, B, EXPERTS])
    chosen = sb("chosen", [P, B, EXPERTS])
    first = sb("first", [P, B])
    run = [sb(f"run{n}", [P, B, EXPERTS]) for n in range(2)]
    rank = sb("rank", [P, B])
    keep = sb("keep", [P, B])
    weight = sb("weight", [P, B])
    slot = sb("slot", [P, B])
    spill = sb("spill", [P, B])
    slot_to = sb("slot_to", [P, B], I32)
    slot_from = sb("slot_from", [P, B], I32)
    rows = sb("ex_rows", [P, 2, CG, D])
    rowsT = sb("ex_rowsT", [P, 2, KC, CAP])
    hidT = sb("ex_hidT", [P, 2, FC, CAP])
    y_rows = sb("y_rows", [P, 2, CG, D])

    weights_in = sem("ex_weights_in")
    w_loaded = [sem(f"ex_w_loaded{n}") for n in range(2)]
    rows_loaded = [sem(f"ex_rows_loaded{n}") for n in range(2)]
    zeros_set = sem("zeros_set")
    zeroed = sem("zeroed")
    ln_done = sem("ex_ln_done")
    rT_ready = sem("rT_ready")
    rT_taken = sem("rT_taken")
    logit_ready = sem("logit_ready")
    logit_taken = sem("logit_taken")
    chosen_ready = sem("chosen_ready")
    ranks_ready = sem("ranks_ready")
    shifted_ready = sem("ex_shifted_ready")
    exp_ready = sem("ex_exp_ready")
    slots_ready = sem("slots_ready")
    scattered = sem("scattered")
    y_stored = [sem(f"y_stored{n}") for n in range(2)]
    gathered = [sem(f"gathered{n}") for n in range(GATHERS)]
    combined = sem("combined")
    stored = sem("stored")
    chain = sem("ex_chain")

    uses = []
    for par in range(2):
        uses += [("T", par, c) for c in range(KC)] + [("F1", par, f) for f in range(FC)] + [("F2", par, t) for t in range(CG)]
    banks = Banks(nc, ctx, "ex", uses, n=5)
    ps_T = [ctx.enter_context(nc.psum_tensor(f"ps_rT{n}", [P, 512], F32)) for n in range(KC)]
    ps_r = ctx.enter_context(nc.psum_tensor("ps_r", [P, 512], F32))

    N_W = 5
    ROUNDS = B // G
    block = ctx.enter_context(nc.Block())

    @block.sync
    def _(sp):
        sp.dma_start(w_r[:, :, :], ins["ex_w_r"].rearrange("(c p) n -> p c n", p=P)).then_inc(weights_in, 16)
        sp.dma_start(before[:, :], ins["before"]).then_inc(weights_in, 16)
        sp.dma_start(ones[:, :], ins["ones"]).then_inc(weights_in, 16)
        sp.dma_start(countdown[:, :], ins["countdown"].to_broadcast([P, EXPERTS])).then_inc(weights_in, 16)
        sp.dma_start(spill_row[:, :], ins["spill_row"]).then_inc(weights_in, 16)

        def load_weights(e, par):
            sp.dma_start(w1[:, par], ins["ex_w1"][bass.ds(e, 1)].rearrange("a (c p) n -> p (a c) n", p=P)
                         ).then_inc(w_loaded[par], 16)
            sp.dma_start(w2[:, par], ins["ex_w2"][bass.ds(e, 1)].rearrange("a (c p) n -> p (a c) n", p=P)
                         ).then_inc(w_loaded[par], 16)

        def load_rows(e, par):
            sp.dma_start(rows[:, par], slots_in[bass.ds(e * CAP, CAP), :].rearrange("(t p) d -> p t d", p=P)
                         ).then_inc(rows_loaded[par], 16)

        load_weights(0, 0)
        load_weights(1, 1)
        sp.wait_ge(zeros_set, 1)
        for n in range(8):
            at = n * SLOTS // 8
            sp.dma_start(slots_in[at:at + SLOTS // 8, :].rearrange("(p a) d -> p (a d)", p=P), zeros[:, :]).then_inc(zeroed, 16)
        sp.wait_ge(scattered, 16 * B)
        load_rows(0, 0)
        load_rows(1, 1)

        def store(r, par):
            n, before_ = banks.count(("F2", par, CG - 1), r)
            sp.wait_ge(banks.taken[n], before_ + 2)
            sp.dma_start(slots_out[bass.ds((2 * r + par) * CAP, CAP), :].rearrange("(t p) d -> p t d", p=P),
                         y_rows[:, par]).then_inc(y_stored[par], 16)

        with sp.Fori(0, EXPERTS // 2 - 1) as r:
            for par in range(2):
                store(r, par)
                load_weights(2 * r + 2 + par, par)
                load_rows(2 * r + 2 + par, par)
        for par in range(2):
            store(EXPERTS // 2 - 1, par)
        for g in range(B // G):
            sp.wait_ge(combined, G * (g + 1))
            sp.dma_start(out[g * G:(g + 1) * G].rearrange("b t d -> t b d"), x_sb[:, g * G:(g + 1) * G, :]).then_inc(stored, 16)
        sp.wait_ge(stored, 16 * (B // G))

    @block.gpsimd
    def _(pool):
        pool.memset(zeros[:, :], 0.0).then_inc(zeros_set, 1)
        pool.wait_ge(zeroed, 16 * 8)
        pool.wait_ge(slots_ready, 1)
        for b in range(B):
            pool.indirect_dma_start(out=slots_in[:, :], out_offset=bass.IndirectOffsetOnAxis(ap=slot_to[:, b:b + 1], axis=0),
                                    in_=xn[:, b, :], in_offset=None).then_inc(scattered, 16)
        for par in range(2):
            pool.wait_ge(y_stored[par], 16 * (EXPERTS // 2 + 1))
        pool.wait_ge(scattered, 16 * B)
        for b in range(B):
            if b >= GATHERS:
                pool.wait_ge(combined, b - GATHERS + 1)
            pool.indirect_dma_start(out=xn[:, b, :], out_offset=None, in_=slots_out[:, :],
                                    in_offset=bass.IndirectOffsetOnAxis(ap=slot_from[:, b:b + 1], axis=0)
                                    ).then_inc(gathered[b % GATHERS], 16)

    @block.tensor
    def _(pe):
        pe.wait_ge(weights_in, 16 * N_W)
        with pe.Fori(0, ROUNDS) as r:
            pe.wait_ge(logit_taken, r + 1)
            pe.wait_ge(ln_done, r + 1)
            for c in range(KC):
                for g in range(G):
                    mm = pe.transpose(ps_T[c][:, g * T:(g + 1) * T], xn_group[:, g, c * P:(c + 1) * P], ident[:, :])
            mm.then_inc(rT_ready, 1)
            pe.wait_ge(rT_taken, r + 1)
            for g in range(G):
                for c in range(KC):
                    mm = pe.matmul(ps_r[:, g * EXPERTS:(g + 1) * EXPERTS], xnT[:, c, g * T:(g + 1) * T], w_r[:, c, :],
                                   start=(c == 0), stop=(c == KC - 1))
            mm.then_inc(logit_ready, 1)
        pe.wait_ge(chosen_ready, 1)
        flat = chosen[:, :, :].rearrange("p b e -> p (b e)")
        pe.matmul(ps_T[0][:, 0:B * EXPERTS], before[:, :], flat, start=True, stop=True)
        pe.matmul(ps_T[1][:, 0:B * EXPERTS], ones[:, :], flat, start=True, stop=True).then_inc(ranks_ready, 1)

        with pe.Fori(0, EXPERTS // 2) as r:
            def open_bank(use):
                n, before_ = banks.count(use, r)
                pe.wait_ge(banks.taken[n], before_ + 1)
                return banks.ps[n], banks.ready[n]

            def taken(use):
                n, before_ = banks.count(use, r)
                pe.wait_ge(banks.taken[n], before_ + 2)

            for par in range(2):
                pe.wait_ge(rows_loaded[par], 16 * (r + 1))
                for c in range(KC):
                    ps, ready = open_bank(("T", par, c))
                    for t in range(CG):
                        mm = pe.transpose(ps[:, t * P:(t + 1) * P], rows[:, par, t, c * P:(c + 1) * P], ident[:, :])
                    mm.then_inc(ready, 1)
                pe.wait_ge(w_loaded[par], 32 * (r + 1))
                for f in range(FC):
                    ps, ready = open_bank(("F1", par, f))
                    if f == 0:
                        taken(("T", par, KC - 1))
                    for c in range(KC):
                        mm = pe.matmul(ps[:, :], w1[:, par, c, f * P:(f + 1) * P], rowsT[:, par, c, :],
                                       start=(c == 0), stop=(c == KC - 1))
                    mm.then_inc(ready, 1)
                for t in range(CG):
                    ps, ready = open_bank(("F2", par, t))
                    if t == 0:
                        taken(("F1", par, FC - 1))
                    for f in range(FC):
                        mm = pe.matmul(ps[:, 0:D], hidT[:, par, f, t * P:(t + 1) * P], w2[:, par, f, :],
                                       start=(f == 0), stop=(f == FC - 1))
                    mm.then_inc(ready, 1)

    @block.scalar
    def _(act):
        with act.Fori(0, ROUNDS) as r:
            act.wait_ge(rT_ready, r + 1)
            for c in range(KC):
                last = act.activation(xnT[:, c, :], ps_T[c][:, :], ACT.Copy)
            last.then_inc(rT_taken, 1)
        act.wait_ge(shifted_ready, 1)
        act.activation(expd[:, :, :], expd[:, :, :], ACT.Exp).then_inc(exp_ready, 1)
        with act.Fori(0, EXPERTS // 2) as r:
            def take(use):
                n, before_ = banks.count(use, r)
                act.wait_ge(banks.ready[n], before_ + 1)
                return banks.ps[n], banks.taken[n]

            for par in range(2):
                for c in range(KC):
                    ps, taken = take(("T", par, c))
                    act.activation(rowsT[:, par, c, :], ps[:, :], ACT.Copy).then_inc(taken, 1)
                for f in range(FC):
                    ps, taken = take(("F1", par, f))
                    act.activation(hidT[:, par, f, :], ps[:, :], ACT.Relu).then_inc(taken, 1)

    @block.vector
    def _(dve):
        dve.wait_ge(weights_in, 16 * N_W)
        for n in range(banks.n):
            dve.sem_inc(banks.taken[n], 1)
        dve.sem_inc(logit_taken, 1)
        for par in range(2):
            dve.sem_inc(y_stored[par], 16)
        links = [0]
        base = [0]

        def link(ins):
            links[0] += 1
            ins.then_inc(chain, 1)
            dve.wait_ge(chain, base[0] + links[0])

        with dve.Fori(0, ROUNDS) as r:
            base[0] = r * 16
            norm_group(dve, link, x_sb, r, xn_group, ln_done, small)
            dve.wait_ge(ln_done, r + 1)
            dve.tensor_copy(xn[:, bass.ds(r * G, G), :], xn_group[:, :, :])
            dve.wait_ge(logit_ready, r + 1)
            dve.tensor_copy(logits[:, bass.ds(r * G, G), :].rearrange("p b e -> p (b e)"),
                            ps_r[:, 0:G * EXPERTS]).then_inc(logit_taken, 1)
        assert links[0] == 16
        base[0], links[0] = 16 * ROUNDS, 0
        dve.wait_ge(logit_taken, ROUNDS + 1)

        def wide(ap):
            return ap.unsqueeze(2).to_broadcast([P, B, EXPERTS])

        order = countdown[:, :].unsqueeze(1).to_broadcast([P, B, EXPERTS])
        link(dve.tensor_reduce(top[:, :], logits[:, :, :], AX.X, ALU.max))
        dve.tensor_tensor(expd[:, :, :], logits[:, :, :], wide(top[:, :]), ALU.subtract).then_inc(shifted_ready, 1)
        link(dve.tensor_tensor(hit[:, :, :], logits[:, :, :], wide(top[:, :]), ALU.is_equal))
        link(dve.tensor_tensor(hit[:, :, :], hit[:, :, :], order, ALU.mult))
        link(dve.tensor_reduce(first[:, :], hit[:, :, :], AX.X, ALU.max))
        dve.tensor_tensor(chosen[:, :, :], order, wide(first[:, :]), ALU.is_equal).then_inc(chosen_ready, 1)
        dve.wait_ge(exp_ready, 1)
        link(dve.tensor_reduce(weight[:, :], expd[:, :, :], AX.X, ALU.add))
        link(dve.reciprocal(weight[:, :], weight[:, :]))
        dve.wait_ge(ranks_ready, 1)
        totals = ps_T[1][:, 0:B * EXPERTS].rearrange("p (b e) -> p b e", e=EXPERTS)
        dve.memset(run[0][:, 0:1, :], 0.0)
        link(dve.tensor_copy(run[0][:, 1:B, :], totals[:, 0:B - 1, :]))
        step, cur = 1, 0
        while step < B:
            dve.tensor_copy(run[1 - cur][:, 0:step, :], run[cur][:, 0:step, :])
            link(dve.tensor_tensor(run[1 - cur][:, step:B, :], run[cur][:, step:B, :], run[cur][:, 0:B - step, :], ALU.add))
            step, cur = 2 * step, 1 - cur
        within = ps_T[0][:, 0:B * EXPERTS].rearrange("p (b e) -> p b e", e=EXPERTS)
        link(dve.tensor_tensor(hit[:, :, :], within, run[cur][:, :, :], ALU.add))
        link(dve.tensor_tensor(hit[:, :, :], hit[:, :, :], chosen[:, :, :], ALU.mult))
        link(dve.tensor_reduce(rank[:, :], hit[:, :, :], AX.X, ALU.add))
        dve.tensor_scalar(keep[:, :], rank[:, :], float(CAP), None, ALU.is_lt)
        link(dve.scalar_tensor_tensor(slot[:, :], first[:, :], -float(CAP), rank[:, :], ALU.mult, ALU.add))
        link(dve.tensor_scalar(slot[:, :], slot[:, :], float(SLOTS), None, ALU.add))
        link(dve.tensor_tensor(spill[:, :], slot[:, :], spill_row[:, :], ALU.subtract))
        link(dve.tensor_tensor(spill[:, :], spill[:, :], keep[:, :], ALU.mult))
        dve.tensor_tensor(slot_to[:, :], spill[:, :], spill_row[:, :], ALU.add)
        dve.tensor_tensor(weight[:, :], weight[:, :], keep[:, :], ALU.mult)
        dve.tensor_tensor(slot_from[:, :], slot[:, :], keep[:, :], ALU.mult).then_inc(slots_ready, 1)

        with dve.Fori(0, EXPERTS // 2) as r:
            for par in range(2):
                for t in range(CG):
                    n, before_ = banks.count(("F2", par, t), r)
                    dve.wait_ge(banks.ready[n], before_ + 1)
                    if t == 0:
                        dve.wait_ge(y_stored[par], 16 * (r + 1))
                    dve.tensor_copy(y_rows[:, par, t, :], banks.ps[n][:, 0:D]).then_inc(banks.taken[n], 1)
        for b in range(B):
            dve.wait_ge(gathered[b % GATHERS], 16 * (b // GATHERS + 1))
            dve.scalar_tensor_tensor(x_sb[:, b, :], xn[:, b, :], weight[:, b:b + 1], x_sb[:, b, :], ALU.mult,
                                     ALU.add).then_inc(combined, 1)


def program(nc, ins, outs):
    with ExitStack() as ctx:
        def sb(name, shape, dt=F32):
            return ctx.enter_context(nc.sbuf_tensor(name, shape, dt))

        x_sb = sb("x_sb", [P, B, D])
        ident = sb("ident", [P, P])
        causal = sb("causal", [P, T])
        head_masks = sb("head_masks", [P, 4])
        with ExitStack() as part:
            transformer(nc, part, x_sb, ins, (ident, causal, head_masks))
        with ExitStack() as part:
            linear_attention(nc, part, x_sb, ins, (ident,))
        with ExitStack() as part:
            experts(nc, part, x_sb, ins, (ident,), outs[0])


_OUTS = [((B, T, D), "float32")]


def lay_out(inputs):
    import numpy as np

    def tok(name):
        return np.ascontiguousarray(inputs["L0_tok_" + name])

    def cols(a):
        return a.reshape(a.shape[0], -1, P).transpose(0, 2, 1)

    a = {"idxT": np.asarray(inputs["x"]).T, "tok_emb": tok("tok_emb"), "pos_emb": tok("pos_emb")}
    for name in ("wq", "wk", "wv", "w_proj", "w1", "w2", "b_proj", "b2"):
        a[name] = tok(name)
    a["b1_cols"] = cols(tok("b1"))
    a["ln1_cols"] = np.concatenate([cols(tok("ln1_w")), cols(tok("ln1_b"))], axis=2)
    a["ln2_cols"] = np.concatenate([cols(tok("ln2_w")), cols(tok("ln2_b"))], axis=2)
    row = np.arange(P)
    a["ident"] = np.eye(P, dtype=np.float32)
    a["causal"] = np.where(row[None, :] > row[:, None], MASKED, 0.0).astype(np.float32)
    a["head_masks"] = (row[:, None] // HD % 4 == np.arange(4)[None, :]).astype(np.float32)

    def la(name):
        return np.asarray(inputs["L0_attn_" + name])

    a["la_w_in"] = la("W_in").T
    parts = la("W_qkva").reshape(D, 4, 2, D)
    bias = la("b_qkva").reshape(D, 4, 2)
    at = {"q": 0, "k": 1, "v": 2, "a": 3, "re": 0, "im": 1}
    a["la_w_comp"] = np.concatenate([parts[:, at[c[0]], at[c[1:]], :].T for c in COMPS], axis=1)
    v_rows = parts[:, 2].reshape(LA_HEADS, LA_D, 2, D).transpose(3, 0, 2, 1)
    a["la_w_v"] = v_rows.reshape(D, 2 * D)
    a["la_v_bias"] = bias[:, 2].reshape(LA_HEADS, LA_D, 2).transpose(0, 2, 1).reshape(1, 2 * D)
    a["la_w_y"] = la("W_y").reshape(D, LA_HEADS, LA_D, 2).transpose(3, 1, 2, 0).reshape(2 * D, D)
    a["la_w_out"] = la("W_out").T
    a["la_out_bias"] = la("b_out").reshape(1, D)
    columns = [bias[:, at[c[0]], at[c[1:]]] for c in COMPS] + [la("b_in"), la("b_y")]
    a["la_bias_cols"] = np.concatenate([c.reshape(KC, P).T for c in columns], axis=1)
    h0 = np.zeros((TILES, 2, 2, LA_D, 2, LA_D), np.float32)
    for n, name in enumerate(("h0_re", "h0_im")):
        for h in range(LA_HEADS):
            h0[h // 2, h % 2, n, :, h % 2, :] = la(name)[h]
    a["la_h0"] = h0.reshape(TILES, P, 2 * LA_D).transpose(1, 0, 2)
    masks = np.zeros((P, MASK_LEVELS, T // 2), np.uint32)
    for n, m in enumerate(LEVELS[:MASK_LEVELS]):
        for j in range(T // 2):
            block = j // m
            masks[2 * m * block:2 * m * block + m, n, j] = 1
    a["la_masks"] = masks

    a["ex_w_r"] = np.asarray(inputs["L0_ffn_Wr"])
    a["ex_w1"] = np.asarray(inputs["L0_ffn_W1"])
    a["ex_w2"] = np.asarray(inputs["L0_ffn_W2"])
    a["before"] = (row[:, None] < row[None, :]).astype(np.float32)
    a["ones"] = np.ones((P, P), np.float32)
    a["countdown"] = np.arange(EXPERTS, 0, -1, dtype=np.float32)[None]
    a["spill_row"] = (SLOTS + T * np.arange(B)[None, :] + row[:, None]).astype(np.float32)
    return {k: np.ascontiguousarray(v) for k, v in a.items()}


def kernel(**inputs):
    import numpy as _np
    import concourse.bacc as _bacc
    from concourse import mybir as _mybir
    from concourse.bass_utils import run_bass_kernel_spmd as _run

    nc = _bacc.Bacc("TRN2", target_bir_lowering=False, num_devices=1)
    arrays, ins = {}, {}
    for name, a in lay_out(inputs).items():
        arrays[f"in_{name}_dram"] = a
        ins[name] = nc.dram_tensor(f"in_{name}_dram", a.shape, _mybir.dt.from_np(a.dtype), kind="ExternalInput").ap()
    outs = [nc.dram_tensor(f"out_{i}_dram", shape, _mybir.dt.from_np(_np.dtype(dtype)), kind="ExternalOutput").ap()
            for i, (shape, dtype) in enumerate(_OUTS)]
    program(nc, ins, outs)
    r = _run(nc, [arrays], core_ids=[0])
    return r.results[0]["out_0_dram"]
```
